# Optimizing a Trainium2 kernel written in Bass

```python
import numpy as np
import jax
import jax.numpy as jnp

def _softmax(x, axis=-1):
    return jax.nn.softmax(x, axis=axis)

def _gelu(x):
    return jax.nn.gelu(x, approximate=True)

def _silu(x):
    return jax.nn.silu(x)

def _sigmoid(x):
    return jax.nn.sigmoid(x)

def _layernorm(x, axis=-1, eps=1e-05):
    m = jnp.mean(x, axis=axis, keepdims=True)
    v = jnp.var(x, axis=axis, keepdims=True)
    return (x - m) / jnp.sqrt(v + eps)

def _scatter_add(tgt, idx, src, axis=0):
    return tgt.at[idx].add(src)

def _segment_sum(src, seg, n):
    return jax.ops.segment_sum(src, seg, n)
kernel_name = 'mk_adj_ffn_d1_adj_r2_494dba'

def setup_inputs(seed: int=0):
    np.random.seed(seed)
    _w = jnp.asarray

    def _rec_inputs():
        import jax
        import jax.numpy as jnp
        _gk = jax.random.key(seed)
        x = -0.0002928 + 1 * jax.random.normal(jax.random.fold_in(_gk, 1), (32, 256, 256), jnp.float32)
        _a = jax.random.bernoulli(jax.random.fold_in(_gk, 2), 0.0625, (32, 256, 256))
        adj = _a.astype(jnp.int32)
        return (x, adj)
    x, adj = _rec_inputs()

    def _L0_gnn_setup():
        import jax, jax.numpy as jnp
        import numpy as np
        NEG_SLOPE = 0.2
        key = jax.random.key(seed)
        k1, k2, k3, k4, k5 = jax.random.split(key, 5)
        B, N, H = (8, 512, 256)
        node_features = jax.random.normal(k1, (B, N, H), dtype=jnp.float32)
        adjacency_matrix = jax.random.randint(k2, (B, N, N), 0, 2, dtype=jnp.int32)
        scale = 1.0 / np.sqrt(2 * H)
        attn_w_src = jax.random.uniform(k3, (H,), jnp.float32, -scale, scale)
        attn_w_dst = jax.random.uniform(k4, (H,), jnp.float32, -scale, scale)
        attn_b = jax.random.uniform(k5, (1,), jnp.float32, -scale, scale)
        return {'node_features': node_features, 'adjacency_matrix': adjacency_matrix, 'attn_w_src': attn_w_src, 'attn_w_dst': attn_w_dst, 'attn_b': attn_b}
    _L0_gnn_all = _L0_gnn_setup()
    _L0_gnn_in = {k: v for k, v in _L0_gnn_all.items() if k in ('attn_w_src', 'attn_w_dst', 'attn_b')}
    del _L0_gnn_all

    def _L0_ffn_setup():
        import jax, jax.numpy as jnp
        import numpy as np
        H = 256
        FF = 4 * H
        E = 8
        K = 2
        B, S = (4, 2048)
        key = jax.random.key(seed)
        ks = jax.random.split(key, 4)
        s = 0.02
        return {'x': jax.random.normal(ks[0], (B, S, H), dtype=jnp.float32), 'Wg': jax.random.normal(ks[1], (H, E), dtype=jnp.float32) * s, 'bg': jnp.zeros((E,), dtype=jnp.float32), 'W1': jax.random.normal(ks[2], (E, H, FF), dtype=jnp.float32) * s, 'b1': jnp.zeros((E, FF), dtype=jnp.float32), 'W2': jax.random.normal(ks[3], (E, FF, H), dtype=jnp.float32) * s, 'b2': jnp.zeros((E, H), dtype=jnp.float32)}
    _L0_ffn_all = _L0_ffn_setup()
    _L0_ffn_in = {k: v for k, v in _L0_ffn_all.items() if k in ('Wg', 'bg', 'W1', 'b1', 'W2', 'b2')}
    del _L0_ffn_all
    return {'x': x, 'adj': adj, 'L0_gnn_attn_w_src': _L0_gnn_in['attn_w_src'], 'L0_gnn_attn_w_dst': _L0_gnn_in['attn_w_dst'], 'L0_gnn_attn_b': _L0_gnn_in['attn_b'], 'L0_ffn_Wg': _L0_ffn_in['Wg'], 'L0_ffn_bg': _L0_ffn_in['bg'], 'L0_ffn_W1': _L0_ffn_in['W1'], 'L0_ffn_b1': _L0_ffn_in['b1'], 'L0_ffn_W2': _L0_ffn_in['W2'], 'L0_ffn_b2': _L0_ffn_in['b2']}

def reference(x, adj, L0_gnn_attn_w_src, L0_gnn_attn_w_dst, L0_gnn_attn_b, L0_ffn_Wg, L0_ffn_bg, L0_ffn_W1, L0_ffn_b1, L0_ffn_W2, L0_ffn_b2):
    import jax
    import jax.numpy as jnp

    def _L0_gnn_ref(node_features, adjacency_matrix, attn_w_src, attn_w_dst, attn_b):
        import jax, jax.numpy as jnp
        import numpy as np
        NEG_SLOPE = 0.2
        B, N, H = node_features.shape
        s_src = jnp.einsum('bnh,h->bn', node_features, attn_w_src)
        s_dst = jnp.einsum('bnh,h->bn', node_features, attn_w_dst)
        scores = s_src[:, :, None] + s_dst[:, None, :] + attn_b[0]
        scores = jax.nn.leaky_relu(scores, negative_slope=NEG_SLOPE)
        adj = adjacency_matrix.astype(jnp.float32) + jnp.eye(N, dtype=jnp.float32)[None]
        scores = jnp.where(adj == 0, -jnp.inf, scores)
        attn = jax.nn.softmax(scores, axis=-1)
        return jnp.einsum('bij,bjh->bih', attn, node_features)

    def _L0_ffn_ref(x, Wg, bg, W1, b1, W2, b2):
        import jax, jax.numpy as jnp
        import numpy as np
        H = 256
        FF = 4 * H
        E = 8
        K = 2
        B, S = (4, 2048)
        logits = x @ Wg + bg
        w, idx = jax.lax.top_k(logits, K)
        w = jax.nn.softmax(w, axis=-1)
        h = jax.nn.silu(jnp.einsum('bsh,ehf->ebsf', x, W1) + b1[:, None, None, :])
        y = jnp.einsum('ebsf,efh->ebsh', h, W2) + b2[:, None, None, :]
        comb = jnp.einsum('bske,bsk->ebs', jax.nn.one_hot(idx, E, dtype=x.dtype), w)
        return jnp.einsum('ebsh,ebs->bsh', y, comb)
    x = x + _L0_gnn_ref(_layernorm(x, axis=-1), adj, L0_gnn_attn_w_src, L0_gnn_attn_w_dst, L0_gnn_attn_b)
    x = x + _L0_ffn_ref(_layernorm(x, axis=-1), L0_ffn_Wg, L0_ffn_bg, L0_ffn_W1, L0_ffn_b1, L0_ffn_W2, L0_ffn_b2)
    return x

_drawn_inputs = setup_inputs


def setup_inputs(seed=0):
    import zlib

    import numpy as np

    out = dict(_drawn_inputs(seed))
    spreads = {'L0_ffn_bg': (0.0, 0.1), 'L0_ffn_b1': (0.0, 0.35), 'L0_ffn_b2': (0.0, 0.1)}
    factors = {}
    for name, (base, spread) in spreads.items():
        noise = np.random.default_rng([zlib.crc32(name.encode()), seed]).standard_normal(out[name].shape)
        drawn = base * np.exp(spread * noise) if base else spread * noise
        out[name] = jnp.asarray(drawn.astype(out[name].dtype))
    for name, factor in factors.items():
        out[name] = (out[name] * factor).astype(out[name].dtype)
    return out
```

```python
from contextlib import ExitStack

import concourse.bass as bass
from concourse import mybir

F32 = mybir.dt.float32
F16 = mybir.dt.float16
BF16 = mybir.dt.bfloat16
I32 = mybir.dt.int32
ALU = mybir.AluOpType
ACT = mybir.ActivationFunctionType
AX = mybir.AxisListType

P = 128
GRAPHS = 32
N = 256
H = 256
E = 8
FF = 1024
RB = N // P
KT = H // P
FT = FF // P
TOKENS = GRAPHS * N
TRASH = P
TILE = 256
SUB = TILE // P
TILES = (2 * TOKENS) // TILE + E - 1
REGION = TOKENS + TILE
NULL_BASE = E * REGION
WORDS = H + 4
EPS = 1e-5
SLOPE = 0.2
BIG = 1e30
WSCALE = 256.0
MAGIC = 1597463007.0
U = 8
BATCH = 4
COLS = BATCH * RB
HALF = KT * FF
LN_STEPS = 13
STAGES = 40


class At:

    def __init__(self, unit, m, o):
        self.unit, self.m, self.o = unit, m, o
        self.i = unit * m + o

    def back(self, n):
        return At(self.unit, self.m, self.o - n)

    def slot(self, n):
        return self.o % n

    def turn(self, n):
        return (self.unit // n) * self.m + self.o // n

    def within(self, n):
        return not isinstance(self.i, int) or 0 <= self.i < n

    def past(self, n):
        return not isinstance(self.i, int) or self.i >= n


def capped(value, n):
    return min(value, n) if isinstance(value, int) else value


def build_gat_moe(nc, x, adj, w_src, w_dst, attn_b, w_gate, b_gate, w1, b1, w2, b2, out):
    rows = nc.dram_tensor("expert_rows", [NULL_BASE + TILE, WORDS], F32, kind="Internal").ap()
    x_rows = x.rearrange("g (r p) h -> g p r h", p=P)
    adj_rows = adj.rearrange("g (r p) n -> g p r n", p=P)
    out_rows = out[0:TOKENS, :].rearrange("(g r p) h -> g p r h", r=RB, p=P)
    w1_rows = w1.rearrange("e (k p) f -> e p k f", p=P)
    w2_rows = w2.rearrange("e (t p) h -> e p t h", p=P)

    ctx = ExitStack()
    with ctx:
        def sb(name, shape, dt):
            return ctx.enter_context(nc.sbuf_tensor(name, shape, dt))[tuple(slice(0, n) for n in shape)]

        def sem(name):
            return ctx.enter_context(nc.semaphore(name))

        ctx.enter_context(nc.allow_non_contiguous_dma(reason="a few small vectors"))
        ctx.enter_context(nc.allow_low_precision(reason="places are whole numbers below 2^24"))

        W = sb("W", [P, E * 4 * HALF], F16)
        arena_at = [4 * 4 * HALF]

        def arena(words, dt=F32):
            a = arena_at[0]
            arena_at[0] += 2 * words
            assert arena_at[0] <= E * 4 * HALF
            v = W[:, a:a + 2 * words]
            return v if dt == F16 else v.bitcast(dt)

        xb = [arena(RB * H).rearrange("p (r h) -> p r h", r=RB) for _ in range(8)]
        adjb = [arena(RB * N, I32).rearrange("p (r n) -> p r n", r=RB) for _ in range(4)]
        nf = [arena(RB * (H + 2)).rearrange("p (r h) -> p r h", r=RB) for _ in range(4)]
        nfT = [arena(KT * N).rearrange("p (k n) -> p k n", k=KT) for _ in range(2)]
        noedge = [arena(RB * N // 2, BF16).rearrange("p (r n) -> p r n", r=RB) for _ in range(2)]
        diag = [arena(RB * P).rearrange("p (j n) -> p j n", j=RB) for _ in range(2)]
        e1_both = arena(2 * RB * N)
        e1 = [e1_both[:, i * RB * N:(i + 1) * RB * N].rearrange("p (r n) -> p r n", r=RB) for i in range(2)]
        e2 = [arena(RB * N).rearrange("p (r n) -> p r n", r=RB) for _ in range(2)]
        e1T = arena(RB * N).rearrange("p (j n) -> p j n", j=RB)
        probsT = [arena(RB * N).rearrange("p (j n) -> p j n", j=RB) for _ in range(2)]
        x2 = [arena(RB * H).rearrange("p (r h) -> p r h", r=RB) for _ in range(2)]

        xnT = [arena(KT * N).rearrange("p (k n) -> p k n", k=KT) for _ in range(2)]

        row_region = sb("row_region", [P, 2 * COLS * WORDS], F32)
        rowbuf = row_region[:, :].rearrange("p (c w) -> p c w", w=WORDS)
        x2 += [sb(f"x2_{i}", [P, RB, H], F32) for i in range(2)]
        stage = [sb(f"stage{i}", [P, HALF], F32) for i in range(2)]

        hparts = row_region[:, 0:2 * 2 * FT * TILE // 2].bitcast(F16)\
            .rearrange("p (b q f n) -> p b q f n", b=2, q=2, f=FT)
        hid = [[hparts[:, b, q, :, :] for q in range(2)] for b in range(2)]
        xr = [sb(f"xr{i}", [P, SUB, WORDS], F32) for i in range(2)]
        xTh = [sb(f"xTh{i}", [P, KT, TILE], F16) for i in range(2)]
        xTl = [sb(f"xTl{i}", [P, KT, TILE], F16) for i in range(2)]
        act = [sb(f"act{i}", [P, 2, TILE], F32) for i in range(2)]
        ysum = [sb(f"ysum{i}", [P, SUB, H], F32) for i in range(2)]
        yout = [sb(f"yout{i}", [P, SUB, H], F32) for i in range(2)]
        place_tok = [sb(f"place_tok{i}", [P, SUB], I32) for i in range(2)]
        place_w = [sb(f"place_w{i}", [P, SUB], F32) for i in range(2)]
        place_q = sb("place_q", [P, SUB], F32)

        ident = sb("ident", [P, P], F32)
        ones = sb("ones", [P, P], F32)
        ones_bf = sb("ones_bf", [P, P], BF16)
        minus_big = sb("minus_big", [P, P], BF16)
        before = sb("before", [P, P], BF16)
        minus_eye = sb("minus_eye", [P, RB, N], F32)
        rank = sb("rank", [P, COLS, E], F32)
        expert_no = sb("expert_no", [P, E + 1], F32)
        tile_no = sb("tile_no", [P, TILES], F32)
        template = sb("template", [P, SUB, WORDS], F32)
        w_sd = sb("w_sd", [P, KT, 2], F32)
        wg_sb = sb("wg_sb", [P, KT, E], F32)
        bg_sb = sb("bg_sb", [P, RB, E], F32)
        attn_b_sb = sb("attn_b_sb", [P, 1], F32)
        ad_bias = sb("ad_bias", [P, RB, 2], F32)
        b1_rows = sb("b1_rows", [E * FT, P], F32)
        b1T = sb("b1T", [P, E * FT], F32)
        b2_sb = sb("b2_sb", [P, E, H], F32)

        stat1 = sb("stat1", [P, RB, 6], F32)
        stat2 = sb("stat2", [P, RB, 6], F32)
        mv = [sb(f"mv{i}", [P, 2 * RB, 2], F32) for i in range(2)]
        rstd = [sb(f"rstd{i}", [P, 2 * RB], F32) for i in range(2)]
        shift2 = [sb(f"shift2_{i}", [P, RB], F32) for i in range(2)]
        nv = sb("nv", [P, 2 * RB], F32)
        nhalf = sb("nhalf", [P, 2 * RB], F32)
        ny = sb("ny", [P, 2 * RB], F32)
        nt = sb("nt", [P, 2 * RB], F32)
        ad = [sb(f"ad{i}", [P, RB, 2], F32) for i in range(2)]
        rmax = sb("rmax", [P, RB], F32)
        rz = sb("rz", [P, RB], F32)
        rm = sb("rm", [P, RB], F32)
        ebias = [sb(f"ebias{i}", [P, 2, RB], F32) for i in range(2)]
        rinv = sb("rinv", [P, RB], F32)
        lg = sb("lg", [P, COLS, E], F32)
        lg2 = sb("lg2", [P, COLS, E], F32)
        hit = sb("hit", [P, COLS, E], F32)
        first = sb("first", [P, COLS, E], F32)
        second = sb("second", [P, COLS, E], F32)
        top1 = sb("top1", [P, COLS], F32)
        top2 = sb("top2", [P, COLS], F32)
        rank1 = sb("rank1", [P, COLS], F32)
        rank2 = sb("rank2", [P, COLS], F32)
        sel = sb("sel", [P, COLS, E], BF16)
        gate_e = sb("gate_e", [P, COLS], F32)
        gate_w1 = sb("gate_w1", [P, COLS], F32)
        slot_f = sb("slot_f", [P, COLS, E], F32)
        slot_s = sb("slot_s", [P, COLS, E], F32)
        slot_1 = sb("slot_1", [P, 2 * COLS], I32)
        slot_2 = sb("slot_2", [P, 2 * COLS], I32)
        free_at = sb("free_at", [P, E], F32)
        cnt_i = sb("cnt_i", [P, E], I32)
        tiles_i = sb("tiles_i", [P, E], I32)
        tiles_f = sb("tiles_f", [P, E], F32)
        tile_end = sb("tile_end", [P, E], F32)
        coef = sb("coef", [P, E + 1], F32)
        past = e1_both[:, 0:TILES * (E + 1)].rearrange("p (t e) -> p t e", e=E + 1)
        tile_e = sb("tile_e", [P, TILES], F32)
        tile_rank = sb("tile_rank", [P, TILES], F32)
        tile_b = sb("tile_b", [P, TILES], F32)
        region_end = sb("region_end", [P, E], I32)
        tile_expert = sb("tile_expert", [P, TILES], I32)
        tile_base = sb("tile_base", [P, TILES], I32)

        bank = [ctx.enter_context(nc.psum_tensor(f"bank{i}", [P, 512], F32)) for i in range(4)]
        o_ps = ctx.enter_context(nc.psum_tensor("o_ps", [P, RB, 512], F32))
        bank += [None, None] + [ctx.enter_context(nc.psum_tensor(f"bank{i}", [P, 512], F32)) for i in (6, 7)]
        nfT_ps = bank[0][:, :].rearrange("p (k n) -> p k n", k=KT)
        s_ps = bank[1][:, :].rearrange("p (r n) -> p r n", r=RB)
        e1T_ps = bank[2][:, :].rearrange("p (j n) -> p j n", j=RB)
        e2T_ps = bank[3][:, :].rearrange("p (j n) -> p j n", j=RB)
        xnT_ps = bank[6][:, :].rearrange("p (k n) -> p k n", k=KT)
        small = bank[7]
        ad_ps = small[:, 0:RB * 2].rearrange("p (r a) -> p r a", r=RB)
        lg_ps = small[:, 16:16 + RB * E].rearrange("p (r e) -> p r e", r=RB)
        pre_ps = small[:, 64:64 + COLS * E].rearrange("p (c e) -> p c e", c=COLS)
        tot_ps = small[:, 128:128 + E]
        b1T_ps = small[:, 256:256 + E * FT]
        xT_ps = bank[0][:, :].rearrange("p (k n) -> p k n", k=KT)
        h_ps = [bank[1], bank[2], bank[3], bank[6]]
        h_ps = [b[:, :].rearrange("p (f n) -> p f n", f=2) for b in h_ps]
        y_ps = [o_ps[:, i, :].rearrange("p (s h) -> p s h", s=SUB) for i in range(2)]

        x_in = [sem(f"x_in{i}") for i in range(8)]
        adj_in = [sem(f"adj_in{i}") for i in range(4)]
        x2_stored = [sem(f"x2_stored{i}") for i in range(4)]
        scatter_done = [sem(f"scatter_done{i}") for i in range(8)]
        vectors_in = sem("vectors_in")
        const_steps = sem("const_steps")
        vconst_done = sem("vconst_done")
        trash_zeroed = sem("trash_zeroed")
        b1_turned = sem("b1_turned")
        b1_ready = sem("b1_ready")
        stats1_steps = sem("stats1_steps")
        stats2_steps = sem("stats2_steps")
        root_steps = sem("root_steps")
        nf_ready = sem("nf_ready")
        nfT_ready = sem("nfT_ready")
        nfT_copied = sem("nfT_copied")
        ad_ready = sem("ad_ready")
        ad_copied = sem("ad_copied")
        diag_ready = sem("diag_ready")
        mask_ready = sem("mask_ready")
        scores_ready = sem("scores_ready")
        rowmax_steps = sem("rowmax_steps")
        exp_ready = sem("exp_ready")
        e1T_ready = sem("e1T_ready")
        e2T_ready = sem("e2T_ready")
        e1T_copied = sem("e1T_copied")
        probsT_ready = sem("probsT_ready")
        attn_ready = sem("attn_ready")
        x2_steps = sem("x2_steps")
        xn_ready = sem("xn_ready")
        xnT_ready = sem("xnT_ready")
        xnT_copied = sem("xnT_copied")
        logits_ready = sem("logits_ready")
        logits_copied = sem("logits_copied")
        choose_steps = sem("choose_steps")
        prefix_ready = sem("prefix_ready")
        gate_exp = sem("gate_exp")
        rows_free = sem("rows_free")
        place_steps = sem("place_steps")
        plan_steps = sem("plan_steps")
        padded = sem("padded")
        w_in = [sem(f"w_in{i}") for i in range(2)]
        w_hi = sem("w_hi")
        w_lo = sem("w_lo")
        xr_in = [sem(f"xr_in{i}") for i in range(2)]
        xT_ready = sem("xT_ready")
        xT_hi = sem("xT_hi")
        xT_lo = sem("xT_lo")
        hidden_ready = sem("hidden_ready")
        silu_ready = sem("silu_ready")
        parts_steps = sem("parts_steps")
        y_ready = sem("y_ready")
        ysum_ready = sem("ysum_ready")
        weight_steps = sem("weight_steps")
        yout_ready = sem("yout_ready")
        tok_copied = sem("tok_copied")
        added = sem("added")
        passed = {k: sem(f"passed_{k}") for k in ("pe", "act", "dve", "pool", "sp")}

        def settle(eng, who):
            eng.sem_inc(passed[who], 1)

        CONSTS = 21
        CHOOSE = 14
        PLACE = 13
        PLAN = 19

        def ticks(eng, tick):
            for k in range(U):
                tick(At(U, 0, k))
            with eng.Fori(1, GRAPHS // U) as m:
                for k in range(U):
                    tick(At(U, m, k))
            for k in range(GRAPHS, STAGES):
                tick(At(U, k // U, k % U))

        SPLIT_STEPS = 2 * ((E - 2 + 1) // 2) + 1
        TURNS = (TILES - SPLIT_STEPS) // 2 - 1
        assert SPLIT_STEPS + 2 * TURNS + 2 == TILES

        def steps(eng, step):
            for t in range(SPLIT_STEPS):
                step(At(2, 0, t))
            with eng.Fori(0, TURNS) as m:
                for o in range(2):
                    step(At(2, m, SPLIT_STEPS + o))
            for t in range(TILES - 2, TILES + 2):
                step(At(2, 0, t))

        def w_at(e, part):
            return (e * 4 + part) * HALF

        block = ctx.enter_context(nc.Block())

        @block.sync
        def _(sp):
            def load_x(g):
                if g.within(GRAPHS):
                    if g.past(8):
                        sp.wait_ge(x2_steps, 3 * (g.i - 7))
                    settle(sp, "sp")
                    sp.dma_start(xb[g.slot(8)], x_rows[bass.ds(g.i, 1)].rearrange("g p r h -> (g p) r h"))\
                        .then_inc(x_in[g.slot(8)], 16)

            def load_adj(g):
                if g.within(GRAPHS):
                    if g.past(4):
                        sp.wait_ge(mask_ready, g.i - 3)
                    settle(sp, "sp")
                    sp.dma_start(adjb[g.slot(4)], adj_rows[bass.ds(g.i, 1)].rearrange("g p r n -> (g p) r n"))\
                        .then_inc(adj_in[g.slot(4)], 16)

            def store_x2(g):
                if g.within(GRAPHS):
                    sp.wait_ge(x2_steps, 3 * (g.i + 1))
                    settle(sp, "sp")
                    sp.dma_start(out_rows[bass.ds(g.i, 1)].rearrange("g p r h -> (g p) r h"), x2[g.slot(4)])\
                        .then_inc(x2_stored[g.slot(4)], 16)

            def load_w(q):
                if q >= 2:
                    sp.wait_ge(w_lo, q - 1)
                src = w1_rows if q % 2 == 0 else w2_rows
                sp.dma_start(stage[q % 2][:, :].rearrange("p (k f) -> p k f", k=KT if q % 2 == 0 else FT),
                             src[q // 2]).then_inc(w_in[q % 2], 16)

            load_x(At(U, 0, 0))
            load_adj(At(U, 0, 0))
            sp.dma_start(w_sd[:, :, 0], w_src.rearrange("(k p) -> p k", p=P)).then_inc(vectors_in, 16)
            sp.dma_start(w_sd[:, :, 1], w_dst.rearrange("(k p) -> p k", p=P)).then_inc(vectors_in, 16)
            sp.dma_start(attn_b_sb[:, :], attn_b.rearrange("(a n) -> a n", a=1).to_broadcast((P, 1)))\
                .then_inc(vectors_in, 16)
            sp.dma_start(wg_sb[:, :, :], w_gate.rearrange("(k p) e -> p k e", p=P)).then_inc(vectors_in, 16)
            for r in range(RB):
                sp.dma_start(bg_sb[:, r, :], b_gate.rearrange("(a n) -> a n", a=1).to_broadcast((P, E)))\
                    .then_inc(vectors_in, 16)
            sp.dma_start(b1_rows[:, :], b1.rearrange("e (t p) -> (e t) p", p=P)).then_inc(vectors_in, 16)
            sp.dma_start(b2_sb[:, :, :].rearrange("p e h -> p (e h)"),
                         b2.rearrange("(a e) h -> a (e h)", a=1).to_broadcast((P, E * H))).then_inc(vectors_in, 16)

            def tick(k):
                store_x2(k.back(8))
                if not (isinstance(k.i, int) and k.i == 0):
                    load_x(k)
                g = k.back(3)
                if not (isinstance(g.i, int) and g.i == 0):
                    load_adj(g)
                if isinstance(k.i, int) and k.i == U - 1:
                    load_w(0)
                    load_w(1)
                    sp.wait_ge(vconst_done, 1)
                    sp.dma_start(out[TOKENS:TOKENS + TRASH, :], template[:, 0, 0:H]).then_inc(trash_zeroed, 16)
                if isinstance(k.i, int) and k.i == GRAPHS + 2:
                    sp.wait_ge(const_steps, CONSTS)
                    sp.dma_start(rows[NULL_BASE:NULL_BASE + TILE, :].rearrange("(s p) w -> p s w", p=P),
                                 template[:, :, :]).then_inc(padded, 16)
            ticks(sp, tick)
            load_w(2)
            load_w(3)
            sp.wait_ge(plan_steps, PLAN)
            for e in range(E):
                end = sp.value_load(region_end[0:1, e:e + 1], min_val=e * REGION, max_val=e * REGION + TOKENS)
                sp.dma_start(rows[bass.ds(end, TILE), :].rearrange("(s p) w -> p s w", p=P),
                             template[:, :, :]).then_inc(padded, 16)
            sp.wait_ge(padded, 16 * (E + 1))
            for s in scatter_done:
                sp.wait_ge(s, 64 * GRAPHS // 8)

            def step(t):
                if t.within(TILES):
                    base = sp.value_load(tile_base[0:1, bass.ds(t.i, 1)], min_val=0, max_val=NULL_BASE)
                    if t.past(2):
                        sp.wait_ge(weight_steps, 2 * (t.i - 1))
                    if t.past(2):
                        sp.wait_ge(xT_ready, t.i - 1)
                    if t.past(2):
                        sp.wait_ge(tok_copied, t.i - 1)
                    settle(sp, "sp")
                    sp.dma_start(xr[t.slot(2)][:, :, :],
                                 rows[bass.ds(base, TILE), :].rearrange("(s p) w -> p s w", p=P))\
                        .then_inc(xr_in[t.slot(2)], 16)
                if isinstance(t.i, int) and t.i < E - 2:
                    load_w(2 * (t.i + 2))
                    load_w(2 * (t.i + 2) + 1)
            steps(sp, step)

        @block.gpsimd
        def _(pool):
            done = [0]

            def const(ins):
                done[0] += 1
                ins.then_inc(const_steps, 1)
                pool.wait_ge(const_steps, done[0])

            const(nc.gpsimd.memset(ident[:, :], 0.0))
            const(nc.gpsimd.affine_select(out=ident[:, :], in_=ident[:, :], compare_op=ALU.not_equal, fill=1.0,
                                          base=0, pattern=[[-1, P]], channel_multiplier=1))
            const(nc.gpsimd.memset(ones[:, :], 1.0))
            const(nc.gpsimd.memset(minus_eye[:, :, :], 0.0))
            const(nc.gpsimd.affine_select(out=minus_eye[:, :, :], in_=minus_eye[:, :, :], compare_op=ALU.not_equal,
                                          fill=-1.0, base=0, pattern=[[P, RB], [-1, N]], channel_multiplier=1))
            for i in range(4):
                const(nc.gpsimd.memset(nf[i][:, :, H:H + 1], 1.0))
            const(nc.gpsimd.memset(ones_bf[:, :], 1.0))
            const(nc.gpsimd.memset(minus_big[:, :], 0.0))
            const(nc.gpsimd.affine_select(out=minus_big[:, :], in_=minus_big[:, :], compare_op=ALU.not_equal,
                                          fill=-BIG, base=0, pattern=[[-1, P]], channel_multiplier=1))
            const(nc.gpsimd.affine_select(out=before[:, :], in_=ones_bf[:, :], compare_op=ALU.is_gt, fill=0.0,
                                          base=0, pattern=[[1, P]], channel_multiplier=-1))
            const(nc.gpsimd.iota(rank[:, :, :], pattern=[[0, COLS], [-1, E]], base=E, channel_multiplier=0,
                                 allow_small_or_imprecise_dtypes=True))
            const(nc.gpsimd.iota(expert_no[:, :], pattern=[[1, E + 1]], base=0, channel_multiplier=0,
                                 allow_small_or_imprecise_dtypes=True))
            const(nc.gpsimd.iota(tile_no[:, :], pattern=[[1, TILES]], base=0, channel_multiplier=0,
                                 allow_small_or_imprecise_dtypes=True))
            const(nc.gpsimd.iota(free_at[:, :], pattern=[[REGION, E]], base=0, channel_multiplier=0,
                                 allow_small_or_imprecise_dtypes=True))
            const(nc.gpsimd.iota(coef[:, :], pattern=[[REGION, E + 1]], base=0, channel_multiplier=0,
                                 allow_small_or_imprecise_dtypes=True))
            const(nc.gpsimd.iota(rowbuf[:, :, H:H + 1].bitcast(I32), pattern=[[P, 2 * COLS], [0, 1]],
                                 base=-2 * BATCH * N, channel_multiplier=1))
            pool.wait_ge(vconst_done, 1)
            const(nc.gpsimd.iota(template[:, 0, H:H + 1].bitcast(I32), pattern=[[0, 1]], base=TOKENS,
                                 channel_multiplier=1))
            const(nc.gpsimd.iota(template[:, 1, H:H + 1].bitcast(I32), pattern=[[0, 1]], base=TOKENS,
                                 channel_multiplier=1))
            assert done[0] == CONSTS, done

            def normalise(g):
                if g.within(GRAPHS):
                    pool.wait_ge(root_steps, LN_STEPS * (g.i + 1))
                    if g.past(4):
                        pool.wait_ge(attn_ready, g.i - 3)
                    settle(pool, "pool")
                    p = g.slot(2)
                    for r in range(RB):
                        nc.gpsimd.tensor_scalar(nf[g.slot(4)][:, r, 0:H], xb[g.slot(8)][:, r, :],
                                                mv[p][:, r, 0:1], rstd[p][:, r:r + 1],
                                                ALU.subtract, ALU.mult).then_inc(nf_ready, 1)

            def spread(g):
                if g.within(GRAPHS):
                    pool.wait_ge(ad_copied, g.i + 1)
                    if g.past(2):
                        pool.wait_ge(scores_ready, g.i - 1)
                    settle(pool, "pool")
                    for j in range(RB):
                        nc.gpsimd.tensor_scalar(diag[g.slot(2)][:, j, :], ident[:, :], ad[g.slot(2)][:, j, 1:2], None,
                                                ALU.mult).then_inc(diag_ready, 1)

            def scatter(g):
                if g.within(GRAPHS):
                    pool.wait_ge(xn_ready, 2 * (g.i + 1))
                    pool.wait_ge(place_steps, PLACE * (g.turn(BATCH) + 1))
                    settle(pool, "pool")
                    for r in range(RB):
                        c = RB * g.slot(8) + r
                        for places in (slot_1, slot_2):
                            nc.gpsimd.indirect_dma_start(rows, bass.IndirectOffsetOnAxis(ap=places[:, c:c + 1], axis=0),
                                                         rowbuf[:, c, :], None).then_inc(scatter_done[g.slot(8)], 16)

            def free(g):
                if g.within(GRAPHS):
                    pool.wait_ge(scatter_done[g.slot(8)], 64 * (g.turn(8) + 1))
                    pool.sem_inc(rows_free, 1)

            def tick(k):
                normalise(k)
                spread(k.back(1))
                scatter(k.back(8))
                free(k.back(8))
            pool.sem_inc(rows_free, 8)
            ticks(pool, tick)

            for i, s in enumerate(x2_stored):
                pool.wait_ge(s, 16 * GRAPHS // 4)
            pool.wait_ge(trash_zeroed, 16)

            def step(t):
                v = t.back(2)
                if v.within(TILES):
                    pool.wait_ge(yout_ready, 2 * (v.i + 1))
                    pool.wait_ge(tok_copied, v.i + 1)
                    settle(pool, "pool")
                    for s in range(SUB):
                        nc.gpsimd.indirect_dma_start(
                            out, bass.IndirectOffsetOnAxis(ap=place_tok[v.slot(2)][:, s:s + 1], axis=0),
                            yout[v.slot(2)][:, s, :], None, compute_op=ALU.add).then_inc(added, 16)
                        pool.wait_ge(added, 16 * (SUB * v.i + s + 1))
                        settle(pool, "pool")
                if t.within(TILES):
                    pool.wait_ge(xr_in[t.slot(2)], 16 * (t.turn(2) + 1))
                    settle(pool, "pool")
                    nc.gpsimd.tensor_copy(place_tok[t.slot(2)][:, :], xr[t.slot(2)][:, :, H].bitcast(I32))\
                        .then_inc(tok_copied, 1)
            steps(pool, step)

        @block.scalar
        def _(sc):
            nc_act = nc.scalar.activation

            def exps(g):
                if g.within(GRAPHS):
                    sc.wait_ge(rowmax_steps, 5 * (g.i + 1))
                    if g.past(2):
                        sc.wait_ge(e2T_ready, g.i - 1)
                    for r in range(RB):
                        nc_act(e1[g.slot(2)][:, r, :], s_ps[:, r, :], ACT.Exp,
                               bias=ebias[g.slot(2)][:, 0, r:r + 1]).then_inc(exp_ready, 1)
                        nc_act(e2[g.slot(2)][:, r, :], s_ps[:, r, :], ACT.Exp,
                               bias=ebias[g.slot(2)][:, 1, r:r + 1], scale=SLOPE).then_inc(exp_ready, 1)

            def copy_nfT(g):
                if g.within(GRAPHS):
                    sc.wait_ge(nfT_ready, g.i + 1)
                    if g.past(2):
                        sc.wait_ge(ad_ready, g.i - 1)
                    nc_act(nfT[g.slot(2)], nfT_ps, ACT.Copy).then_inc(nfT_copied, 1)

            def copy_e1T(g):
                if g.within(GRAPHS):
                    sc.wait_ge(e1T_ready, g.i + 1)
                    if g.past(1):
                        sc.wait_ge(probsT_ready, g.i)
                    nc_act(e1T, e1T_ps, ACT.Copy).then_inc(e1T_copied, 1)

            def normalise2(g):
                if g.within(GRAPHS):
                    sc.wait_ge(root_steps, LN_STEPS * (g.i + 4))
                    sc.wait_ge(rows_free, g.i + 1)
                    p = (g.o + 3) % 2
                    for r in range(RB):
                        nc_act(rowbuf[:, RB * g.slot(8) + r, 0:H], x2[g.slot(4)][:, r, :], ACT.Identity,
                               bias=shift2[p][:, r:r + 1], scale=rstd[p][:, RB + r:RB + r + 1]).then_inc(xn_ready, 1)

            def copy_xnT(g):
                if g.within(GRAPHS):
                    sc.wait_ge(xnT_ready, g.i + 1)
                    if g.past(2):
                        sc.wait_ge(logits_ready, g.i - 1)
                    nc_act(xnT[g.slot(2)], xnT_ps, ACT.Copy).then_inc(xnT_copied, 1)

            def gate(b):
                sc.wait_ge(choose_steps, CHOOSE * (b + 1))
                nc_act(gate_e[:, :], gate_e[:, :], ACT.Exp).then_inc(gate_exp, 1)

            def split_hi(q):
                sc.wait_ge(w_in[q % 2], 16 * (q // 2 + 1))
                if q // 2 >= 4:
                    sc.wait_ge(plan_steps, PLAN)
                    for s in x2_stored:
                        sc.wait_ge(s, 16 * GRAPHS // 4)
                a = w_at(q // 2, 2 * (q % 2))
                nc_act(W[:, a:a + HALF], stage[q % 2][:, :], ACT.Copy, scale=WSCALE).then_inc(w_hi, 1)

            def tick(k):
                normalise2(k.back(4))
                copy_nfT(k.back(1))
                exps(k.back(2))
                copy_xnT(k.back(4))
                copy_e1T(k.back(2))
                b = k.back(8)
                if k.o % BATCH == 0 and b.within(GRAPHS):
                    gate(b.turn(BATCH))
            sc.wait_ge(const_steps, 3)
            nc_act(gate_e[:, 0:1], ones[:, 0:1], ACT.Exp).then_inc(passed["act"], 1)
            sc.wait_ge(passed["act"], 1)
            ticks(sc, tick)
            for q in range(4):
                split_hi(q)

            def x_hi(t):
                if t.within(TILES):
                    sc.wait_ge(xT_ready, t.i + 1)
                    if t.past(2):
                        sc.wait_ge(hidden_ready, 4 * (t.i - 1))
                    nc_act(xTh[t.slot(2)][:, :, :], xT_ps, ACT.Copy).then_inc(xT_hi, 1)

            def silu(t):
                if t.within(TILES):
                    e = sc.value_load(tile_expert[0:1, bass.ds(t.i, 1)], min_val=0, max_val=E - 1)
                    for j in range(4):
                        sc.wait_ge(hidden_ready, 4 * t.i + j + 1)
                        if j > 1 or t.past(1):
                            sc.wait_ge(parts_steps, 2 * (4 * t.i + j - 1))
                        settle(sc, "act")
                        for f in range(2):
                            ins = nc_act(act[j % 2][:, f, :], h_ps[j][:, f, :], ACT.Silu,
                                         bias=b1T[:, bass.ds(e * FT + 2 * j + f, 1)], scale=1.0 / WSCALE)
                        ins.then_inc(silu_ready, 1)

            def weigh(t):
                if t.within(TILES):
                    sc.wait_ge(ysum_ready, t.i + 1)
                    sc.wait_ge(weight_steps, 2 * (t.i + 1))
                    if t.past(2):
                        sc.wait_ge(added, 32 * (t.i - 1))
                    for s in range(SUB):
                        nc_act(yout[t.slot(2)][:, s, :], ysum[t.slot(2)][:, s, :], ACT.Copy,
                               scale=place_w[t.slot(2)][:, s:s + 1]).then_inc(yout_ready, 1)

            sc.wait_ge(b1_ready, 1)
            sc.wait_ge(plan_steps, PLAN)
            nc_act(gate_e[:, 0:1], ones[:, 0:1], ACT.Silu).then_inc(passed["act"], 1)
            x_hi(At(2, 0, 0))

            def step(t):
                weigh(t.back(2))
                silu(t)
                x_hi(t.back(-1))
                if isinstance(t.i, int) and t.i < E - 2:
                    split_hi(2 * (t.i + 2))
                    split_hi(2 * (t.i + 2) + 1)
            steps(sc, step)

        @block.vector
        def _(dve):
            v = nc.vector
            v.memset(template[:, :, :], 0.0).then_inc(vconst_done, 1)
            for i in range(2):
                v.memset(mv[i][:, :, :], 1.0).then_inc(vconst_done, 1)
            v.memset(ad_bias[:, :, :], 0.0).then_inc(vconst_done, 1)
            dve.wait_ge(vconst_done, 4)
            dve.wait_ge(vectors_in, 16 * 8)
            v.tensor_copy(ad_bias[:, :, 0], attn_b_sb[:, 0:1].to_broadcast((P, RB))).then_inc(vconst_done, 1)
            dve.wait_ge(vconst_done, 5)
            dve.wait_ge(const_steps, CONSTS)
            dve.wait_ge(b1_turned, 1)
            v.tensor_copy(b1T[:, :], b1T_ps).then_inc(b1_ready, 1)

            def stats1(g):
                if g.within(GRAPHS):
                    dve.wait_ge(x_in[g.slot(8)], 16 * (g.turn(8) + 1))
                    if g.past(1):
                        dve.wait_ge(stats1_steps, 4 * g.i)
                    for r in range(RB):
                        v.bn_stats(stat1[:, r, :], xb[g.slot(8)][:, r, :]).then_inc(stats1_steps, 1)
                    dve.wait_ge(stats1_steps, 4 * g.i + 2)
                    if g.past(2):
                        dve.wait_ge(nf_ready, 2 * (g.i - 1))
                    settle(dve, "dve")
                    for r in range(RB):
                        v.bn_aggr(mv[g.slot(2)][:, r, :], stat1[:, r, :]).then_inc(stats1_steps, 1)

            def stats2(g):
                if g.within(GRAPHS):
                    dve.wait_ge(x2_steps, 3 * (g.i + 1))
                    if g.past(1):
                        dve.wait_ge(stats2_steps, 4 * g.i)
                    for r in range(RB):
                        v.bn_stats(stat2[:, r, :], x2[g.slot(4)][:, r, :]).then_inc(stats2_steps, 1)
                    dve.wait_ge(stats2_steps, 4 * g.i + 2)
                    settle(dve, "dve")
                    for r in range(RB):
                        v.bn_aggr(mv[(g.o + 3) % 2][:, RB + r, :], stat2[:, r, :]).then_inc(stats2_steps, 1)

            def roots(k):
                if not k.within(GRAPHS + 3):
                    return
                n = [0]

                def link(ins):
                    n[0] += 1
                    ins.then_inc(root_steps, 1)
                    dve.wait_ge(root_steps, LN_STEPS * k.i + n[0])

                p = k.slot(2)
                dve.wait_ge(stats1_steps, 4 * capped(k.i + 1, GRAPHS))
                if k.past(3):
                    dve.wait_ge(stats2_steps, 4 * (k.i - 2))
                link(v.tensor_scalar(nv[:, :], mv[p][:, :, 1], EPS, None, ALU.add))
                link(v.tensor_scalar(nhalf[:, :], nv[:, :], -0.5, None, ALU.mult))
                link(v.tensor_scalar(ny[:, :].bitcast(I32), nv[:, :].bitcast(I32), -0.5, MAGIC, ALU.mult, ALU.add))
                for i in range(3):
                    link(v.tensor_tensor(nt[:, :], ny[:, :], ny[:, :], ALU.mult))
                    link(v.tensor_tensor(nt[:, :], nt[:, :], nhalf[:, :], ALU.mult))
                    if i < 2:
                        link(v.scalar_tensor_tensor(out=ny[:, :], in0=nt[:, :], scalar=1.5, in1=ny[:, :],
                                                    op0=ALU.add, op1=ALU.mult))
                if k.past(2):
                    dve.wait_ge(nf_ready, 2 * capped(k.i - 1, GRAPHS))
                if k.past(5):
                    dve.wait_ge(xn_ready, 2 * (k.i - 4))
                link(v.scalar_tensor_tensor(out=rstd[p][:, :], in0=nt[:, :], scalar=1.5, in1=ny[:, :],
                                            op0=ALU.add, op1=ALU.mult))
                link(v.scalar_tensor_tensor(out=shift2[p][:, :], in0=mv[p][:, RB:2 * RB, 0], scalar=-1.0,
                                            in1=rstd[p][:, RB:2 * RB], op0=ALU.mult, op1=ALU.mult))
                assert n[0] == LN_STEPS, n

            def mask(g):
                if g.within(GRAPHS):
                    dve.wait_ge(adj_in[g.slot(4)], 16 * (g.turn(4) + 1))
                    if g.past(2):
                        dve.wait_ge(scores_ready, g.i - 1)
                    v.tensor_tensor(noedge[g.slot(2)], adjb[g.slot(4)], minus_eye[:, :, :], ALU.is_equal)\
                        .then_inc(mask_ready, 1)

            def copy_ad(g):
                if g.within(GRAPHS):
                    dve.wait_ge(ad_ready, g.i + 1)
                    if g.past(2):
                        dve.wait_ge(rowmax_steps, 5 * (g.i - 1))
                    if g.past(2):
                        dve.wait_ge(diag_ready, 2 * (g.i - 1))
                    v.tensor_tensor(ad[g.slot(2)][:, :, :], ad_ps, ad_bias[:, :, :], ALU.add).then_inc(ad_copied, 1)

            def row_max(g):
                if not g.within(GRAPHS):
                    return
                n = [0]

                def link(ins):
                    n[0] += 1
                    ins.then_inc(rowmax_steps, 1)
                    dve.wait_ge(rowmax_steps, 5 * g.i + n[0])

                a = ad[g.slot(2)][:, :, 0]
                dve.wait_ge(ad_copied, g.i + 1)
                dve.wait_ge(scores_ready, g.i + 1)
                link(v.tensor_reduce(rmax[:, :], s_ps, AX.X, ALU.max))
                link(v.tensor_tensor(rz[:, :], rmax[:, :], a, ALU.add))
                link(v.scalar_tensor_tensor(out=rm[:, :], in0=rz[:, :], scalar=SLOPE, in1=rz[:, :],
                                            op0=ALU.mult, op1=ALU.max))
                if g.past(2):
                    dve.wait_ge(exp_ready, 4 * (g.i - 1))
                link(v.tensor_tensor(ebias[g.slot(2)][:, 0, :], a, rm[:, :], ALU.subtract))
                link(v.scalar_tensor_tensor(out=ebias[g.slot(2)][:, 1, :], in0=a, scalar=SLOPE, in1=rm[:, :],
                                            op0=ALU.mult, op1=ALU.subtract))

            def join(g):
                if g.within(GRAPHS):
                    dve.wait_ge(e2T_ready, g.i + 1)
                    dve.wait_ge(e1T_copied, g.i + 1)
                    if g.past(2):
                        dve.wait_ge(attn_ready, g.i - 1)
                    v.tensor_tensor(probsT[g.slot(2)], e2T_ps, e1T, ALU.max).then_inc(probsT_ready, 1)

            def residual(g):
                if g.within(GRAPHS):
                    dve.wait_ge(attn_ready, g.i + 1)
                    if g.past(1):
                        dve.wait_ge(x2_steps, 3 * g.i)
                    v.reciprocal(rinv[:, :], o_ps[:, :, H]).then_inc(x2_steps, 1)
                    dve.wait_ge(x2_steps, 3 * g.i + 1)
                    if g.past(4):
                        dve.wait_ge(x2_stored[g.slot(4)], 16 * g.turn(4))
                    if g.past(4):
                        dve.wait_ge(xn_ready, 2 * (g.i - 3))
                    for r in range(RB):
                        v.scalar_tensor_tensor(out=x2[g.slot(4)][:, r, :], in0=o_ps[:, r, 0:H], scalar=rinv[:, r:r + 1],
                                               in1=xb[g.slot(8)][:, r, :], op0=ALU.mult, op1=ALU.add)\
                            .then_inc(x2_steps, 1)

            def copy_logits(g):
                if g.within(GRAPHS):
                    dve.wait_ge(logits_ready, g.i + 1)
                    c = RB * g.slot(BATCH)
                    v.tensor_tensor(lg[:, c:c + RB, :], lg_ps, bg_sb[:, :, :], ALU.add).then_inc(logits_copied, 1)

            def over_experts(a):
                return a.unsqueeze(2).to_broadcast((P, COLS, E))

            def choose(b):
                n = [0]

                def link(ins):
                    n[0] += 1
                    ins.then_inc(choose_steps, 1)
                    dve.wait_ge(choose_steps, CHOOSE * b + n[0])

                dve.wait_ge(logits_copied, BATCH * (b + 1))
                link(v.tensor_reduce(top1[:, :], lg[:, :, :], AX.X, ALU.max))
                link(v.tensor_tensor(hit[:, :, :], lg[:, :, :], over_experts(top1[:, :]), ALU.is_equal))
                link(v.tensor_tensor(hit[:, :, :], hit[:, :, :], rank[:, :, :], ALU.mult))
                link(v.tensor_reduce(rank1[:, :], hit[:, :, :], AX.X, ALU.max))
                link(v.tensor_tensor(first[:, :, :], rank[:, :, :], over_experts(rank1[:, :]), ALU.is_equal))
                link(v.scalar_tensor_tensor(out=lg2[:, :, :].rearrange("p c e -> p (c e)"),
                                            in0=first[:, :, :].rearrange("p c e -> p (c e)"), scalar=-BIG,
                                            in1=lg[:, :, :].rearrange("p c e -> p (c e)"),
                                            op0=ALU.mult, op1=ALU.add))
                link(v.tensor_reduce(top2[:, :], lg2[:, :, :], AX.X, ALU.max))
                link(v.tensor_tensor(hit[:, :, :], lg2[:, :, :], over_experts(top2[:, :]), ALU.is_equal))
                link(v.tensor_tensor(hit[:, :, :], hit[:, :, :], rank[:, :, :], ALU.mult))
                link(v.tensor_reduce(rank2[:, :], hit[:, :, :], AX.X, ALU.max))
                link(v.tensor_tensor(second[:, :, :], rank[:, :, :], over_experts(rank2[:, :]), ALU.is_equal))
                link(v.tensor_tensor(sel[:, :, :], first[:, :, :], second[:, :, :], ALU.add))
                link(v.tensor_tensor(gate_e[:, :], top2[:, :], top1[:, :], ALU.subtract))
                link(v.tensor_scalar(gate_w1[:, :], rank1[:, :], 1.0, None, ALU.mult))
                assert n[0] == CHOOSE, n

            def place(b, half):
                n = [0]

                def link(ins):
                    n[0] += 1
                    ins.then_inc(place_steps, 1)
                    dve.wait_ge(place_steps, PLACE * b + n[0])

                mine = slice(half * COLS, (half + 1) * COLS)
                dve.wait_ge(gate_exp, b + 1)
                dve.wait_ge(prefix_ready, b + 1)
                link(v.tensor_tensor(slot_f[:, :, :], pre_ps, free_at[:, :].unsqueeze(1).to_broadcast((P, COLS, E)),
                                     ALU.add))
                link(v.tensor_tensor(free_at[:, :], tot_ps, free_at[:, :], ALU.add))
                link(v.tensor_tensor(slot_s[:, :, :], slot_f[:, :, :], first[:, :, :], ALU.mult))
                link(v.tensor_reduce(slot_1[:, mine], slot_s[:, :, :], AX.X, ALU.add))
                link(v.tensor_tensor(slot_s[:, :, :], slot_f[:, :, :], second[:, :, :], ALU.mult))
                link(v.tensor_reduce(slot_2[:, mine], slot_s[:, :, :], AX.X, ALU.add))
                link(v.tensor_copy(rowbuf[:, mine, H + 3], rank1[:, :]))
                link(v.tensor_scalar(gate_w1[:, :], gate_e[:, :], 1.0, None, ALU.add))
                link(v.reciprocal(gate_w1[:, :], gate_w1[:, :]))
                link(v.tensor_tensor(rowbuf[:, mine, H + 1], gate_e[:, :], gate_w1[:, :], ALU.mult))
                link(v.tensor_tensor(rowbuf[:, mine, H + 2], gate_w1[:, :], rowbuf[:, mine, H + 1], ALU.subtract))
                link(v.tensor_scalar(rowbuf[:, mine, H].bitcast(I32), rowbuf[:, mine, H].bitcast(I32),
                                     2 * BATCH * N, None, ALU.add))
                link(v.tensor_copy(top1[:, :], top2[:, :]))
                assert n[0] == PLACE, n

            def tick(k):
                b = k.back(9)
                if k.o % BATCH == 1 and b.within(GRAPHS):
                    half = (b.o // BATCH) % 2
                    place(b.turn(BATCH), half)
                row_max(k.back(2))
                stats1(k)
                copy_logits(k.back(5))
                copy_ad(k.back(1))
                residual(k.back(3))
                stats2(k.back(3))
                roots(k)
                mask(k)
                b = k.back(8)
                if k.o % BATCH == 0 and b.within(GRAPHS):
                    choose(b.turn(BATCH))
                join(k.back(2))
            ticks(dve, tick)

            n = [0]

            def link(ins):
                n[0] += 1
                ins.then_inc(plan_steps, 1)
                dve.wait_ge(plan_steps, n[0])

            def over_tiles(a, width):
                return a.unsqueeze(1).to_broadcast((P, TILES, width))

            link(v.tensor_copy(region_end[:, :], free_at[:, :]))
            link(v.tensor_tensor(tiles_f[:, :], free_at[:, :], coef[:, 0:E], ALU.subtract))
            link(v.tensor_scalar(cnt_i[:, :], tiles_f[:, :], float(TILE - 1), None, ALU.add))
            link(v.tensor_scalar(tiles_i[:, :], cnt_i[:, :], TILE.bit_length() - 1, None, ALU.logical_shift_right))
            link(v.tensor_scalar(tiles_f[:, :], tiles_i[:, :], 1.0, None, ALU.max))
            link(v.tensor_tensor_scan(tile_end[:, :], ones[:, 0:E], tiles_f[:, :], 0.0, ALU.mult, ALU.add))
            link(v.tensor_tensor(tiles_f[:, :], tile_end[:, :], tiles_f[:, :], ALU.subtract))
            link(v.scalar_tensor_tensor(out=coef[:, 0:E], in0=tiles_f[:, :], scalar=-float(TILE), in1=coef[:, 0:E],
                                        op0=ALU.mult, op1=ALU.add))
            link(v.memset(coef[:, E:E + 1], 1e6))
            link(v.tensor_tensor(past[:, :, 0:E], over_tiles(tile_end[:, :], E),
                                 tile_no[:, :].unsqueeze(2).to_broadcast((P, TILES, E)), ALU.is_le))
            link(v.tensor_reduce(tile_e[:, :], past[:, :, 0:E], AX.X, ALU.add))
            link(v.tensor_scalar(tile_rank[:, :], tile_e[:, :], -1.0, float(E), ALU.mult, ALU.add))
            link(v.tensor_scalar(tile_expert[:, :], tile_e[:, :], float(E - 1), None, ALU.min))
            link(v.tensor_tensor(past[:, :, :], over_tiles(expert_no[:, :], E + 1),
                                 tile_e[:, :].unsqueeze(2).to_broadcast((P, TILES, E + 1)), ALU.is_equal))
            link(v.tensor_tensor(past[:, :, :], past[:, :, :], over_tiles(coef[:, :], E + 1), ALU.mult))
            link(v.tensor_reduce(tile_b[:, :], past[:, :, :], AX.X, ALU.add))
            link(v.scalar_tensor_tensor(out=tile_b[:, :], in0=tile_no[:, :], scalar=float(TILE), in1=tile_b[:, :],
                                        op0=ALU.mult, op1=ALU.add))
            link(v.tensor_scalar(tile_base[:, :], tile_b[:, :], float(NULL_BASE), None, ALU.min))
            link(v.tensor_copy(tile_b[:, 0:1], tile_no[:, 0:1]))
            assert n[0] == PLAN, n

            def split_lo(q):
                dve.wait_ge(w_hi, q + 1)
                a = w_at(q // 2, 2 * (q % 2))
                v.scalar_tensor_tensor(out=W[:, a + HALF:a + 2 * HALF], in0=stage[q % 2][:, :], scalar=WSCALE,
                                       in1=W[:, a:a + HALF], op0=ALU.mult, op1=ALU.subtract).then_inc(w_lo, 1)

            for q in range(4):
                split_lo(q)

            def x_lo(t):
                if t.within(TILES):
                    dve.wait_ge(xT_hi, t.i + 1)
                    v.tensor_tensor(xTl[t.slot(2)][:, :, :], xT_ps, xTh[t.slot(2)][:, :, :], ALU.subtract)\
                        .then_inc(xT_lo, 1)

            def parts(t):
                if t.within(TILES):
                    hi, lo = hid[t.slot(2)]
                    if t.past(2):
                        dve.wait_ge(y_ready, t.i - 1)
                    for j in range(4):
                        dve.wait_ge(silu_ready, 4 * t.i + j + 1)
                        pair = slice(2 * j, 2 * j + 2)
                        v.tensor_copy(hi[:, pair, :], act[j % 2][:, :, :]).then_inc(parts_steps, 1)
                        dve.wait_ge(parts_steps, 2 * (4 * t.i + j) + 1)
                        v.tensor_tensor(lo[:, pair, :], act[j % 2][:, :, :], hi[:, pair, :], ALU.subtract)\
                            .then_inc(parts_steps, 1)

            def sum_up(t):
                if t.within(TILES):
                    e = dve.value_load(tile_expert[0:1, bass.ds(t.i, 1)], min_val=0, max_val=E - 1)
                    dve.wait_ge(y_ready, t.i + 1)
                    if t.past(2):
                        dve.wait_ge(yout_ready, 2 * (t.i - 1))
                    v.scalar_tensor_tensor(out=ysum[t.slot(2)][:, :, :], in0=y_ps[t.slot(2)], scalar=1.0 / WSCALE,
                                           in1=b2_sb[:, bass.ds(e, 1), :].to_broadcast((P, SUB, H)),
                                           op0=ALU.mult, op1=ALU.add).then_inc(ysum_ready, 1)

            def weights(t):
                if t.within(TILES):
                    r = xr[t.slot(2)]
                    dve.wait_ge(xr_in[t.slot(2)], 16 * (t.turn(2) + 1))
                    if t.past(1):
                        dve.wait_ge(weight_steps, 2 * t.i)
                    v.scalar_tensor_tensor(out=place_q[:, :], in0=r[:, :, H + 3], scalar=tile_rank[:, bass.ds(t.i, 1)],
                                           in1=r[:, :, H + 2], op0=ALU.is_equal, op1=ALU.mult)\
                        .then_inc(weight_steps, 1)
                    dve.wait_ge(weight_steps, 2 * t.i + 1)
                    if t.past(2):
                        dve.wait_ge(yout_ready, 2 * (t.i - 1))
                    v.tensor_tensor(place_w[t.slot(2)][:, :], place_q[:, :], r[:, :, H + 1], ALU.add)\
                        .then_inc(weight_steps, 1)

            x_lo(At(2, 0, 0))

            def step(t):
                sum_up(t.back(2))
                parts(t)
                x_lo(t.back(-1))
                weights(t)
                if isinstance(t.i, int) and t.i < E - 2:
                    split_lo(2 * (t.i + 2))
                    split_lo(2 * (t.i + 2) + 1)
            steps(dve, step)

        @block.tensor
        def _(pe):
            mm, tp = nc.tensor.matmul, nc.tensor.transpose
            pe.wait_ge(const_steps, CONSTS)
            pe.wait_ge(vectors_in, 16 * 8)
            tp(b1T_ps, b1_rows[:, :], ident[0:E * FT, 0:E * FT]).then_inc(b1_turned, 1)

            def turn_nf(g):
                if g.within(GRAPHS):
                    pe.wait_ge(nf_ready, 2 * (g.i + 1))
                    if g.past(1):
                        pe.wait_ge(nfT_copied, g.i)
                    for r in range(RB):
                        for k in range(KT):
                            ins = tp(nfT_ps[:, k, r * P:(r + 1) * P], nf[g.slot(4)][:, r, k * P:(k + 1) * P],
                                     ident[:, :])
                    ins.then_inc(nfT_ready, 1)

            def attend(g):
                if g.within(GRAPHS):
                    pe.wait_ge(probsT_ready, g.i + 1)
                    if g.past(1):
                        pe.wait_ge(x2_steps, 3 * g.i)
                    for r in range(RB):
                        for j in range(RB):
                            ins = mm(o_ps[:, r, 0:H + 1], probsT[g.slot(2)][:, j, r * P:(r + 1) * P],
                                     nf[g.slot(4)][:, j, 0:H + 1], start=(j == 0), stop=(j == RB - 1))
                    ins.then_inc(attn_ready, 1)

            def node_scores(g):
                if g.within(GRAPHS):
                    pe.wait_ge(nfT_copied, g.i + 1)
                    if g.past(1):
                        pe.wait_ge(ad_copied, g.i)
                    if g.past(4):
                        pe.wait_ge(logits_copied, g.i - 3)
                    if g.o % BATCH == 0 and g.past(8):
                        pe.wait_ge(place_steps, PLACE * capped(g.back(8).turn(BATCH) + 1, GRAPHS // BATCH))
                    for r in range(RB):
                        for k in range(KT):
                            ins = mm(ad_ps[:, r, :], nfT[g.slot(2)][:, k, r * P:(r + 1) * P], w_sd[:, k, :],
                                     start=(k == 0), stop=(k == KT - 1))
                    ins.then_inc(ad_ready, 1)

            def edge_scores(g):
                if g.within(GRAPHS):
                    pe.wait_ge(diag_ready, 2 * (g.i + 1))
                    pe.wait_ge(mask_ready, g.i + 1)
                    if g.past(1):
                        pe.wait_ge(exp_ready, 4 * g.i)
                    for j in range(RB):
                        mm(s_ps[:, :, j * P:(j + 1) * P], ones[:, :],
                           diag[g.slot(2)][:, j, :].unsqueeze(1).to_broadcast((P, RB, P)), start=(j == 0), stop=False)
                    mm(s_ps, minus_big[:, :], noedge[g.slot(2)], start=False, stop=True).then_inc(scores_ready, 1)

            def turn_exps(g):
                if g.within(GRAPHS):
                    pe.wait_ge(exp_ready, 4 * (g.i + 1))
                    if g.past(1):
                        pe.wait_ge(e1T_copied, g.i)
                    if g.past(1):
                        pe.wait_ge(probsT_ready, g.i)
                    for src, dst, ready in ((e1, e1T_ps, e1T_ready), (e2, e2T_ps, e2T_ready)):
                        for r in range(RB):
                            for j in range(RB):
                                ins = tp(dst[:, j, r * P:(r + 1) * P], src[g.slot(2)][:, r, j * P:(j + 1) * P],
                                         ident[:, :])
                        ins.then_inc(ready, 1)

            def turn_xn(g):
                if g.within(GRAPHS):
                    pe.wait_ge(xn_ready, 2 * (g.i + 1))
                    if g.past(1):
                        pe.wait_ge(xnT_copied, g.i)
                    for r in range(RB):
                        for k in range(KT):
                            ins = tp(xnT_ps[:, k, r * P:(r + 1) * P],
                                     rowbuf[:, RB * g.slot(8) + r, k * P:(k + 1) * P], ident[:, :])
                    ins.then_inc(xnT_ready, 1)

            def gate_logits(g):
                if g.within(GRAPHS):
                    pe.wait_ge(xnT_copied, g.i + 1)
                    pe.wait_ge(ad_copied, capped(g.i + 4, GRAPHS))
                    if g.past(1):
                        pe.wait_ge(logits_copied, g.i)
                    for r in range(RB):
                        for k in range(KT):
                            ins = mm(lg_ps[:, r, :], xnT[g.slot(2)][:, k, r * P:(r + 1) * P], wg_sb[:, k, :],
                                     start=(k == 0), stop=(k == KT - 1))
                    ins.then_inc(logits_ready, 1)

            def count(b):
                pe.wait_ge(choose_steps, CHOOSE * b + 12)
                mm(pre_ps, before[:, :], sel[:, :, :], start=True, stop=False)
                for c in range(COLS - 1):
                    mm(pre_ps[:, c + 1:COLS, :], ones_bf[:, :],
                       sel[:, c:c + 1, :].to_broadcast((P, COLS - 1 - c, E)), start=False, stop=(c == COLS - 2))
                for c in range(COLS):
                    ins = mm(tot_ps, ones_bf[:, :], sel[:, c, :], start=(c == 0), stop=(c == COLS - 1))
                ins.then_inc(prefix_ready, 1)

            def tick(k):
                turn_nf(k.back(1))
                attend(k.back(3))
                node_scores(k.back(1))
                turn_xn(k.back(4))
                turn_exps(k.back(2))
                edge_scores(k.back(1))
                gate_logits(k.back(4))
                b = k.back(8)
                if k.o % BATCH == 0 and b.within(GRAPHS):
                    count(b.turn(BATCH))
            ticks(pe, tick)

            def turn_x(t):
                if t.within(TILES):
                    pe.wait_ge(xr_in[t.slot(2)], 16 * (t.turn(2) + 1))
                    if t.past(1):
                        pe.wait_ge(xT_lo, t.i)
                    for s in range(SUB):
                        for k in range(KT):
                            ins = tp(xT_ps[:, k, s * P:(s + 1) * P], xr[t.slot(2)][:, s, k * P:(k + 1) * P],
                                     ident[:, :])
                    ins.then_inc(xT_ready, 1)

            def hidden(t):
                if t.within(TILES):
                    e = pe.value_load(tile_expert[0:1, bass.ds(t.i, 1)], min_val=0, max_val=E - 1)
                    pe.wait_ge(xT_lo, t.i + 1)
                    if isinstance(t.i, int) and t.i < E:
                        pe.wait_ge(w_lo, 2 * (t.i + 1))
                    for j in range(4):
                        if t.past(1):
                            pe.wait_ge(silu_ready, 4 * (t.i - 1) + j + 1)
                        settle(pe, "pe")
                        for f in (2 * j, 2 * j + 1):
                            n = 0
                            for k in range(KT):
                                for part, xT in ((0, xTh), (0, xTl), (1, xTh)):
                                    at = (part * HALF + k * FF + f * P)
                                    ins = mm(h_ps[j][:, f % 2, :], W[:, bass.ds(e * (4 * HALF) + at, P)],
                                             xT[t.slot(2)][:, k, :], start=(n == 0), stop=(n == 5))
                                    n += 1
                        ins.then_inc(hidden_ready, 1)

            def result(t):
                if t.within(TILES):
                    e = pe.value_load(tile_expert[0:1, bass.ds(t.i, 1)], min_val=0, max_val=E - 1)
                    hi, lo = hid[t.slot(2)]
                    pe.wait_ge(parts_steps, 8 * (t.i + 1))
                    if t.past(2):
                        pe.wait_ge(ysum_ready, t.i - 1)
                    for s in range(SUB):
                        n = 0
                        for f in range(FT):
                            for src, part in ((hi, 2), (lo, 2), (hi, 3)):
                                at = part * HALF + f * H
                                ins = mm(y_ps[t.slot(2)][:, s, :], src[:, f, s * P:(s + 1) * P],
                                         W[:, bass.ds(e * (4 * HALF) + at, H)], start=(n == 0), stop=(n == 3 * FT - 1))
                                n += 1
                    ins.then_inc(y_ready, 1)

            pe.wait_ge(plan_steps, PLAN)
            turn_x(At(2, 0, 0))

            def step(t):
                hidden(t)
                turn_x(t.back(-1))
                result(t.back(1))
            steps(pe, step)


_INS = ["x", "adj", "L0_gnn_attn_w_src", "L0_gnn_attn_w_dst", "L0_gnn_attn_b", "L0_ffn_Wg", "L0_ffn_bg",
        "L0_ffn_W1", "L0_ffn_b1", "L0_ffn_W2", "L0_ffn_b2"]


def kernel(**inputs):
    import numpy as _np
    import concourse.bacc as _bacc
    from concourse import mybir as _mybir
    from concourse.bass_utils import run_bass_kernel_spmd as _run

    nc = _bacc.Bacc("TRN2", target_bir_lowering=False, num_devices=1)
    arrays, args = {}, []
    for name in _INS:
        a = _np.ascontiguousarray(inputs[name])
        arrays[f"in_{name}_dram"] = a
        args.append(nc.dram_tensor(f"in_{name}_dram", a.shape, _mybir.dt.from_np(a.dtype), kind="ExternalInput").ap())
    out = nc.dram_tensor("out_0_dram", (TOKENS + TRASH, H), F32, kind="ExternalOutput").ap()
    build_gat_moe(nc, *args, out)
    r = _run(nc, [arrays], core_ids=[0])
    return r.results[0]["out_0_dram"][:TOKENS].reshape(GRAPHS, N, H)
```

```python
from contextlib import ExitStack

import concourse.bass as bass
from concourse import mybir

F32 = mybir.dt.float32
F16 = mybir.dt.float16
BF16 = mybir.dt.bfloat16
I32 = mybir.dt.int32
ALU = mybir.AluOpType
ACT = mybir.ActivationFunctionType
AX = mybir.AxisListType

P = 128
GRAPHS = 32
N = 256
H = 256
E = 8
FF = 1024
RB = N // P
KT = H // P
FT = FF // P
TOKENS = GRAPHS * N
TRASH = P
TILE = 256
SUB = TILE // P
TILES = (2 * TOKENS) // TILE + E - 1
REGION = TOKENS + TILE
NULL_BASE = E * REGION
WORDS = H + 4
EPS = 1e-5
SLOPE = 0.2
BIG = 1e30
WSCALE = 256.0
U = 8
BATCH = 4
COLS = BATCH * RB
HALF = KT * FF
STAGES = 45


class At:

    def __init__(self, unit, m, o):
        self.unit, self.m, self.o = unit, m, o
        self.i = unit * m + o

    def back(self, n):
        return At(self.unit, self.m, self.o - n)

    def slot(self, n):
        return self.o % n

    def turn(self, n):
        return (self.unit // n) * self.m + self.o // n

    def within(self, n):
        return not isinstance(self.i, int) or 0 <= self.i < n

    def past(self, n):
        return not isinstance(self.i, int) or self.i >= n


def capped(value, n):
    return min(value, n) if isinstance(value, int) else value


def build_gat_moe(nc, x, adj, w_src, w_dst, attn_b, w_gate, b_gate, w1, b1, w2, b2, out):
    rows = nc.dram_tensor("expert_rows", [NULL_BASE + TILE, WORDS], F32, kind="Internal").ap()
    x_rows = x.rearrange("g (r p) h -> g p r h", p=P)
    adj_rows = adj.rearrange("g (r p) n -> g p r n", p=P)
    out_rows = out[0:TOKENS, :].rearrange("(g r p) h -> g p r h", r=RB, p=P)
    w1_rows = w1.rearrange("e (k p) f -> e p k f", p=P)
    w2_rows = w2.rearrange("e (t p) h -> e p t h", p=P)

    ctx = ExitStack()
    with ctx:
        def sb(name, shape, dt):
            return ctx.enter_context(nc.sbuf_tensor(name, shape, dt))[tuple(slice(0, n) for n in shape)]

        def sem(name):
            return ctx.enter_context(nc.semaphore(name))

        ctx.enter_context(nc.allow_non_contiguous_dma(reason="a few small vectors"))
        ctx.enter_context(nc.allow_low_precision(reason="places are whole numbers below 2^24"))

        W = sb("W", [P, E * 4 * HALF], F16)
        arena_at = [4 * 4 * HALF]

        def arena(words, dt=F32):
            a = arena_at[0]
            arena_at[0] += 2 * words
            assert arena_at[0] <= E * 4 * HALF
            v = W[:, a:a + 2 * words]
            return v if dt == F16 else v.bitcast(dt)

        xb = [arena(RB * H).rearrange("p (r h) -> p r h", r=RB) for _ in range(8)]
        adjb = [arena(RB * N, I32).rearrange("p (r n) -> p r n", r=RB) for _ in range(4)]
        nf = [arena(RB * (H + 2)).rearrange("p (r h) -> p r h", r=RB) for _ in range(4)]
        nfT = [arena(KT * N).rearrange("p (k n) -> p k n", k=KT) for _ in range(2)]
        noedge = [arena(RB * N // 2, BF16).rearrange("p (r n) -> p r n", r=RB) for _ in range(2)]
        diag = [arena(RB * P).rearrange("p (j n) -> p j n", j=RB) for _ in range(2)]
        e1_both = arena(2 * RB * N)
        e1 = [e1_both[:, i * RB * N:(i + 1) * RB * N].rearrange("p (r n) -> p r n", r=RB) for i in range(2)]
        e2 = [arena(RB * N).rearrange("p (r n) -> p r n", r=RB) for _ in range(2)]
        probsT = [arena(RB * N).rearrange("p (j n) -> p j n", j=RB) for _ in range(2)]
        x2 = [arena(RB * H).rearrange("p (r h) -> p r h", r=RB) for _ in range(2)]

        xnT = [arena(KT * N).rearrange("p (k n) -> p k n", k=KT) for _ in range(2)]

        row_region = sb("row_region", [P, 2 * COLS * WORDS], F32)
        rowbuf = row_region[:, :].rearrange("p (c w) -> p c w", w=WORDS)
        x2 += [sb(f"x2_{i}", [P, RB, H], F32) for i in range(2)]
        stage = [sb(f"stage{i}", [P, HALF], F32) for i in range(2)]

        hparts = row_region[:, 0:2 * 2 * FT * TILE // 2].bitcast(F16)\
            .rearrange("p (b q f n) -> p b q f n", b=2, q=2, f=FT)
        hid = [[hparts[:, b, q, :, :] for q in range(2)] for b in range(2)]
        xr = [sb(f"xr{i}", [P, SUB, WORDS], F32) for i in range(2)]
        xTh = [sb(f"xTh{i}", [P, KT, TILE], F16) for i in range(2)]
        xTl = [sb(f"xTl{i}", [P, KT, TILE], F16) for i in range(2)]
        act = [sb(f"act{i}", [P, 2, TILE], F32) for i in range(2)]
        ysum = [sb(f"ysum{i}", [P, SUB, H], F32) for i in range(2)]
        yout = [sb(f"yout{i}", [P, SUB, H], F32) for i in range(2)]
        place_tok = [sb(f"place_tok{i}", [P, SUB], I32) for i in range(2)]
        place_w = [sb(f"place_w{i}", [P, SUB], F32) for i in range(2)]
        place_q = sb("place_q", [P, SUB], F32)

        ident = sb("ident", [P, P], F32)
        ones = sb("ones", [P, P], F32)
        eps = sb("eps", [P, RB], F32)
        minus_half = sb("minus_half", [P, RB], F32)
        ones_bf = sb("ones_bf", [P, P], BF16)
        minus_big = sb("minus_big", [P, P], BF16)
        before = sb("before", [P, P], BF16)
        minus_eye = sb("minus_eye", [P, RB, N], F32)
        rank = sb("rank", [P, COLS, E], F32)
        expert_no = sb("expert_no", [P, E + 1], F32)
        tile_no = sb("tile_no", [P, TILES], F32)
        template = sb("template", [P, SUB, WORDS], F32)
        w_sd = sb("w_sd", [P, KT, 2], F32)
        wg_sb = sb("wg_sb", [P, KT, E], F32)
        bg_sb = sb("bg_sb", [P, RB, E], F32)
        attn_b_sb = sb("attn_b_sb", [P, 1], F32)
        ad_bias = sb("ad_bias", [P, RB, 2], F32)
        b1_rows = sb("b1_rows", [E * FT, P], F32)
        b1T = sb("b1T", [P, E * FT], F32)
        b2_sb = sb("b2_sb", [P, E, H], F32)

        stat1 = sb("stat1", [P, RB, 6], F32)
        stat2 = sb("stat2", [P, RB, 6], F32)
        mv1 = [sb(f"mv1_{i}", [P, RB, 2], F32) for i in range(2)]
        mv2 = [sb(f"mv2_{i}", [P, RB, 2], F32) for i in range(2)]
        var1 = sb("var1", [P, RB], F32)
        var2 = sb("var2", [P, RB], F32)
        rstd1 = [sb(f"rstd1_{i}", [P, RB], F32) for i in range(2)]
        rstd2 = [sb(f"rstd2_{i}", [P, RB], F32) for i in range(2)]
        shift1 = [sb(f"shift1_{i}", [P, RB], F32) for i in range(2)]
        shift2 = [sb(f"shift2_{i}", [P, RB], F32) for i in range(2)]
        ad = [sb(f"ad{i}", [P, RB, 2], F32) for i in range(2)]
        rmax = sb("rmax", [P, RB], F32)
        rz = sb("rz", [P, RB], F32)
        rm = sb("rm", [P, RB], F32)
        ebias = [sb(f"ebias{i}", [P, 2, RB], F32) for i in range(2)]
        rinv = sb("rinv", [P, RB], F32)
        lg = sb("lg", [P, COLS, E], F32)
        lg2 = sb("lg2", [P, COLS, E], F32)
        hit = sb("hit", [P, COLS, E], F32)
        first = sb("first", [P, COLS, E], F32)
        second = sb("second", [P, COLS, E], F32)
        top1 = sb("top1", [P, COLS], F32)
        top2 = sb("top2", [P, COLS], F32)
        rank1 = sb("rank1", [P, COLS], F32)
        rank2 = sb("rank2", [P, COLS], F32)
        sel = sb("sel", [P, COLS, E], BF16)
        gate_e = sb("gate_e", [P, COLS], F32)
        gate_w1 = sb("gate_w1", [P, COLS], F32)
        slot_f = sb("slot_f", [P, COLS, E], F32)
        slot_s = sb("slot_s", [P, COLS, E], F32)
        slot_1 = sb("slot_1", [P, 2 * COLS], I32)
        slot_2 = sb("slot_2", [P, 2 * COLS], I32)
        free_at = sb("free_at", [P, E], F32)
        cnt_i = sb("cnt_i", [P, E], I32)
        tiles_i = sb("tiles_i", [P, E], I32)
        tiles_f = sb("tiles_f", [P, E], F32)
        tile_end = sb("tile_end", [P, E], F32)
        coef = sb("coef", [P, E + 1], F32)
        past = e1_both[:, 0:TILES * (E + 1)].rearrange("p (t e) -> p t e", e=E + 1)
        tile_e = sb("tile_e", [P, TILES], F32)
        tile_rank = sb("tile_rank", [P, TILES], F32)
        tile_b = sb("tile_b", [P, TILES], F32)
        region_end = sb("region_end", [P, E], I32)
        tile_expert = sb("tile_expert", [P, TILES], I32)
        tile_base = sb("tile_base", [P, TILES], I32)

        bank = [ctx.enter_context(nc.psum_tensor(f"bank{i}", [P, 512], F32)) for i in range(4)]
        o_ps = ctx.enter_context(nc.psum_tensor("o_ps", [P, RB, 512], F32))
        bank += [None, None] + [ctx.enter_context(nc.psum_tensor(f"bank{i}", [P, 512], F32)) for i in (6, 7)]
        nfT_ps = bank[0][:, :].rearrange("p (k n) -> p k n", k=KT)
        s_ps = bank[1][:, :].rearrange("p (r n) -> p r n", r=RB)
        probsT_ps = bank[2][:, :].rearrange("p (j n) -> p j n", j=RB)
        xnT_ps = bank[6][:, :].rearrange("p (k n) -> p k n", k=KT)
        small = bank[7]
        ad_ps = small[:, 0:RB * 2].rearrange("p (r a) -> p r a", r=RB)
        lg_ps = bank[3][:, 0:RB * E].rearrange("p (r e) -> p r e", r=RB)
        pre_ps = bank[3][:, 64:64 + COLS * E].rearrange("p (c e) -> p c e", c=COLS)
        tot_ps = bank[3][:, 128:128 + E]
        b1T_ps = small[:, 256:256 + E * FT]
        xT_ps = bank[0][:, :].rearrange("p (k n) -> p k n", k=KT)
        h_ps = [bank[1], bank[2], bank[3], bank[6]]
        h_ps = [b[:, :].rearrange("p (f n) -> p f n", f=2) for b in h_ps]
        y_ps = [o_ps[:, i, :].rearrange("p (s h) -> p s h", s=SUB) for i in range(2)]

        x_in = [sem(f"x_in{i}") for i in range(8)]
        adj_in = [sem(f"adj_in{i}") for i in range(4)]
        x2_stored = [sem(f"x2_stored{i}") for i in range(4)]
        scatter_done = [sem(f"scatter_done{i}") for i in range(8)]
        vectors_in = sem("vectors_in")
        const_steps = sem("const_steps")
        vconst_done = sem("vconst_done")
        trash_zeroed = sem("trash_zeroed")
        b1_turned = sem("b1_turned")
        b1_ready = sem("b1_ready")
        stats1_steps = sem("stats1_steps")
        stats2_steps = sem("stats2_steps")
        root1_steps = sem("root1_steps")
        root2_steps = sem("root2_steps")
        shift1_ready = sem("shift1_ready")
        shift2_ready = sem("shift2_ready")
        nf_ready = sem("nf_ready")
        nfT_ready = sem("nfT_ready")
        nfT_copied = sem("nfT_copied")
        ad_ready = sem("ad_ready")
        ad_copied = sem("ad_copied")
        diag_ready = sem("diag_ready")
        mask_ready = sem("mask_ready")
        scores_ready = sem("scores_ready")
        rowmax_steps = sem("rowmax_steps")
        exp_ready = sem("exp_ready")
        probs_ready = sem("probs_ready")
        probs_turned = sem("probs_turned")
        probsT_ready = sem("probsT_ready")
        attn_ready = sem("attn_ready")
        x2_steps = sem("x2_steps")
        xn_ready = sem("xn_ready")
        xnT_ready = sem("xnT_ready")
        xnT_copied = sem("xnT_copied")
        logits_ready = sem("logits_ready")
        logits_copied = sem("logits_copied")
        choose_steps = sem("choose_steps")
        prefix_ready = sem("prefix_ready")
        gate_exp = sem("gate_exp")
        rows_free = sem("rows_free")
        place_steps = sem("place_steps")
        plan_steps = sem("plan_steps")
        padded = sem("padded")
        w_in = [sem(f"w_in{i}") for i in range(2)]
        w_hi = sem("w_hi")
        w_lo = sem("w_lo")
        xr_in = [sem(f"xr_in{i}") for i in range(2)]
        xT_ready = sem("xT_ready")
        xT_hi = sem("xT_hi")
        xT_lo = sem("xT_lo")
        hidden_ready = sem("hidden_ready")
        silu_ready = sem("silu_ready")
        parts_steps = sem("parts_steps")
        y_ready = sem("y_ready")
        ysum_ready = sem("ysum_ready")
        weight_steps = sem("weight_steps")
        yout_ready = sem("yout_ready")
        tok_copied = sem("tok_copied")
        added = sem("added")
        passed = {k: sem(f"passed_{k}") for k in ("pe", "act", "dve", "pool", "sp")}

        def settle(eng, who):
            eng.sem_inc(passed[who], 1)

        CONSTS = 23
        CHOOSE = 13
        PLACE = 12
        PLAN = 18

        def ticks(eng, tick):
            for k in range(2 * U):
                tick(At(U, k // U, k % U))
            with eng.Fori(2, GRAPHS // U) as m:
                for k in range(U):
                    tick(At(U, m, k))
            for k in range(GRAPHS, STAGES):
                tick(At(U, k // U, k % U))

        SPLIT_STEPS = 2 * ((E - 2 + 1) // 2) + 1
        TURNS = (TILES - SPLIT_STEPS) // 2 - 1
        assert SPLIT_STEPS + 2 * TURNS + 2 == TILES

        def steps(eng, step):
            for t in range(SPLIT_STEPS):
                step(At(2, 0, t))
            with eng.Fori(0, TURNS) as m:
                for o in range(2):
                    step(At(2, m, SPLIT_STEPS + o))
            for t in range(TILES - 2, TILES + 2):
                step(At(2, 0, t))

        def w_at(e, part):
            return (e * 4 + part) * HALF

        block = ctx.enter_context(nc.Block())

        @block.sync
        def _(sp):
            def load_x(g):
                if g.within(GRAPHS):
                    if g.past(8):
                        sp.wait_ge(x2_steps, 3 * (g.i - 7))
                    settle(sp, "sp")
                    sp.dma_start(xb[g.slot(8)], x_rows[bass.ds(g.i, 1)].rearrange("g p r h -> (g p) r h"))\
                        .then_inc(x_in[g.slot(8)], 16)

            def load_adj(g):
                if g.within(GRAPHS):
                    if g.past(4):
                        sp.wait_ge(mask_ready, g.i - 3)
                    settle(sp, "sp")
                    sp.dma_start(adjb[g.slot(4)], adj_rows[bass.ds(g.i, 1)].rearrange("g p r n -> (g p) r n"))\
                        .then_inc(adj_in[g.slot(4)], 16)

            def store_x2(g):
                if g.within(GRAPHS):
                    sp.wait_ge(x2_steps, 3 * (g.i + 1))
                    settle(sp, "sp")
                    sp.dma_start(out_rows[bass.ds(g.i, 1)].rearrange("g p r h -> (g p) r h"), x2[g.slot(4)])\
                        .then_inc(x2_stored[g.slot(4)], 16)

            def load_w(q):
                if q >= 2:
                    sp.wait_ge(w_lo, q - 1)
                src = w1_rows if q % 2 == 0 else w2_rows
                sp.dma_start(stage[q % 2][:, :].rearrange("p (k f) -> p k f", k=KT if q % 2 == 0 else FT),
                             src[q // 2]).then_inc(w_in[q % 2], 16)

            load_x(At(U, 0, 0))
            load_adj(At(U, 0, 0))
            sp.dma_start(w_sd[:, :, 0], w_src.rearrange("(k p) -> p k", p=P)).then_inc(vectors_in, 16)
            sp.dma_start(w_sd[:, :, 1], w_dst.rearrange("(k p) -> p k", p=P)).then_inc(vectors_in, 16)
            sp.dma_start(attn_b_sb[:, :], attn_b.rearrange("(a n) -> a n", a=1).to_broadcast((P, 1)))\
                .then_inc(vectors_in, 16)
            sp.dma_start(wg_sb[:, :, :], w_gate.rearrange("(k p) e -> p k e", p=P)).then_inc(vectors_in, 16)
            for r in range(RB):
                sp.dma_start(bg_sb[:, r, :], b_gate.rearrange("(a n) -> a n", a=1).to_broadcast((P, E)))\
                    .then_inc(vectors_in, 16)
            sp.dma_start(b1_rows[:, :], b1.rearrange("e (t p) -> (e t) p", p=P)).then_inc(vectors_in, 16)
            sp.dma_start(b2_sb[:, :, :].rearrange("p e h -> p (e h)"),
                         b2.rearrange("(a e) h -> a (e h)", a=1).to_broadcast((P, E * H))).then_inc(vectors_in, 16)

            def tick(k):
                store_x2(k.back(9))
                if not (isinstance(k.i, int) and k.i == 1):
                    load_adj(k.back(1))
                if not (isinstance(k.i, int) and k.i == 0):
                    load_x(k)
                if isinstance(k.i, int) and k.i == U - 1:
                    load_w(0)
                    load_w(1)
                    sp.wait_ge(vconst_done, 1)
                    sp.dma_start(out[TOKENS:TOKENS + TRASH, :], template[:, 0, 0:H]).then_inc(trash_zeroed, 16)
                if isinstance(k.i, int) and k.i == GRAPHS + 2:
                    sp.wait_ge(const_steps, CONSTS)
                    sp.dma_start(rows[NULL_BASE:NULL_BASE + TILE, :].rearrange("(s p) w -> p s w", p=P),
                                 template[:, :, :]).then_inc(padded, 16)
            ticks(sp, tick)
            load_w(2)
            load_w(3)
            sp.wait_ge(plan_steps, PLAN)
            for e in range(E):
                end = sp.value_load(region_end[0:1, e:e + 1], min_val=e * REGION, max_val=e * REGION + TOKENS)
                sp.dma_start(rows[bass.ds(end, TILE), :].rearrange("(s p) w -> p s w", p=P),
                             template[:, :, :]).then_inc(padded, 16)
            sp.wait_ge(padded, 16 * (E + 1))
            for s in scatter_done:
                sp.wait_ge(s, 64 * GRAPHS // 8)

            def step(t):
                if t.within(TILES):
                    base = sp.value_load(tile_base[0:1, bass.ds(t.i, 1)], min_val=0, max_val=NULL_BASE)
                    if t.past(2):
                        sp.wait_ge(weight_steps, 2 * (t.i - 1))
                    if t.past(2):
                        sp.wait_ge(xT_ready, t.i - 1)
                    if t.past(2):
                        sp.wait_ge(tok_copied, t.i - 1)
                    settle(sp, "sp")
                    sp.dma_start(xr[t.slot(2)][:, :, :],
                                 rows[bass.ds(base, TILE), :].rearrange("(s p) w -> p s w", p=P))\
                        .then_inc(xr_in[t.slot(2)], 16)
                if isinstance(t.i, int) and t.i < E - 2:
                    load_w(2 * (t.i + 2))
                    load_w(2 * (t.i + 2) + 1)
            steps(sp, step)

        @block.gpsimd
        def _(pool):
            done = [0]

            def const(ins):
                done[0] += 1
                ins.then_inc(const_steps, 1)
                pool.wait_ge(const_steps, done[0])

            const(nc.gpsimd.memset(ident[:, :], 0.0))
            const(nc.gpsimd.affine_select(out=ident[:, :], in_=ident[:, :], compare_op=ALU.not_equal, fill=1.0,
                                          base=0, pattern=[[-1, P]], channel_multiplier=1))
            const(nc.gpsimd.memset(ones[:, :], 1.0))
            const(nc.gpsimd.memset(eps[:, :], EPS))
            const(nc.gpsimd.memset(minus_half[:, :], -0.5))
            const(nc.gpsimd.memset(minus_eye[:, :, :], 0.0))
            const(nc.gpsimd.affine_select(out=minus_eye[:, :, :], in_=minus_eye[:, :, :], compare_op=ALU.not_equal,
                                          fill=-1.0, base=0, pattern=[[P, RB], [-1, N]], channel_multiplier=1))
            for i in range(4):
                const(nc.gpsimd.memset(nf[i][:, :, H:H + 1], 1.0))
            const(nc.gpsimd.memset(ones_bf[:, :], 1.0))
            const(nc.gpsimd.memset(minus_big[:, :], 0.0))
            const(nc.gpsimd.affine_select(out=minus_big[:, :], in_=minus_big[:, :], compare_op=ALU.not_equal,
                                          fill=-BIG, base=0, pattern=[[-1, P]], channel_multiplier=1))
            const(nc.gpsimd.affine_select(out=before[:, :], in_=ones_bf[:, :], compare_op=ALU.is_gt, fill=0.0,
                                          base=0, pattern=[[1, P]], channel_multiplier=-1))
            const(nc.gpsimd.iota(rank[:, :, :], pattern=[[0, COLS], [-1, E]], base=E, channel_multiplier=0,
                                 allow_small_or_imprecise_dtypes=True))
            const(nc.gpsimd.iota(expert_no[:, :], pattern=[[1, E + 1]], base=0, channel_multiplier=0,
                                 allow_small_or_imprecise_dtypes=True))
            const(nc.gpsimd.iota(tile_no[:, :], pattern=[[1, TILES]], base=0, channel_multiplier=0,
                                 allow_small_or_imprecise_dtypes=True))
            const(nc.gpsimd.iota(free_at[:, :], pattern=[[REGION, E]], base=0, channel_multiplier=0,
                                 allow_small_or_imprecise_dtypes=True))
            const(nc.gpsimd.iota(coef[:, :], pattern=[[REGION, E + 1]], base=0, channel_multiplier=0,
                                 allow_small_or_imprecise_dtypes=True))
            const(nc.gpsimd.iota(rowbuf[:, :, H:H + 1].bitcast(I32), pattern=[[P, 2 * COLS], [0, 1]],
                                 base=-2 * BATCH * N, channel_multiplier=1))
            pool.wait_ge(vconst_done, 1)
            const(nc.gpsimd.iota(template[:, 0, H:H + 1].bitcast(I32), pattern=[[0, 1]], base=TOKENS,
                                 channel_multiplier=1))
            const(nc.gpsimd.iota(template[:, 1, H:H + 1].bitcast(I32), pattern=[[0, 1]], base=TOKENS,
                                 channel_multiplier=1))
            assert done[0] == CONSTS, done

            def root1(g):
                if g.within(GRAPHS):
                    pool.wait_ge(stats1_steps, 4 * (g.i + 1))
                    if g.past(1):
                        pool.wait_ge(root1_steps, 2 * g.i)
                    settle(pool, "pool")
                    nc.gpsimd.tensor_tensor(var1[:, :], mv1[g.slot(2)][:, :, 1], eps[:, :], ALU.add)\
                        .then_inc(root1_steps, 1)
                    pool.wait_ge(root1_steps, 2 * g.i + 1)
                    if g.past(2):
                        pool.wait_ge(nf_ready, 2 * (g.i - 1))
                    settle(pool, "pool")
                    nc.gpsimd.tensor_tensor(rstd1[g.slot(2)][:, :], var1[:, :], minus_half[:, :], ALU.pow)\
                        .then_inc(root1_steps, 1)

            def root2(g):
                if g.within(GRAPHS):
                    pool.wait_ge(stats2_steps, 4 * (g.i + 1))
                    if g.past(1):
                        pool.wait_ge(root2_steps, 2 * g.i)
                    settle(pool, "pool")
                    nc.gpsimd.tensor_tensor(var2[:, :], mv2[g.slot(2)][:, :, 1], eps[:, :], ALU.add)\
                        .then_inc(root2_steps, 1)
                    pool.wait_ge(root2_steps, 2 * g.i + 1)
                    if g.past(2):
                        pool.wait_ge(xn_ready, 2 * (g.i - 1))
                    settle(pool, "pool")
                    nc.gpsimd.tensor_tensor(rstd2[g.slot(2)][:, :], var2[:, :], minus_half[:, :], ALU.pow)\
                        .then_inc(root2_steps, 1)

            def scatter(g):
                if g.within(GRAPHS):
                    pool.wait_ge(xn_ready, 2 * (g.i + 1))
                    pool.wait_ge(place_steps, PLACE * (g.turn(BATCH) + 1))
                    settle(pool, "pool")
                    for r in range(RB):
                        c = RB * g.slot(8) + r
                        for places in (slot_1, slot_2):
                            nc.gpsimd.indirect_dma_start(rows, bass.IndirectOffsetOnAxis(ap=places[:, c:c + 1], axis=0),
                                                         rowbuf[:, c, :], None).then_inc(scatter_done[g.slot(8)], 16)

            def free(g):
                if g.within(GRAPHS):
                    pool.wait_ge(scatter_done[g.slot(8)], 64 * (g.turn(8) + 1))
                    pool.sem_inc(rows_free, 1)

            def tick(k):
                scatter(k.back(13))
                root1(k)
                root2(k.back(5))
                free(k.back(13))
            pool.sem_inc(rows_free, 8)
            ticks(pool, tick)

            for i, s in enumerate(x2_stored):
                pool.wait_ge(s, 16 * GRAPHS // 4)
            pool.wait_ge(trash_zeroed, 16)

            def step(t):
                v = t.back(2)
                if v.within(TILES):
                    pool.wait_ge(yout_ready, 2 * (v.i + 1))
                    pool.wait_ge(tok_copied, v.i + 1)
                    settle(pool, "pool")
                    for s in range(SUB):
                        nc.gpsimd.indirect_dma_start(
                            out, bass.IndirectOffsetOnAxis(ap=place_tok[v.slot(2)][:, s:s + 1], axis=0),
                            yout[v.slot(2)][:, s, :], None, compute_op=ALU.add).then_inc(added, 16)
                        pool.wait_ge(added, 16 * (SUB * v.i + s + 1))
                        settle(pool, "pool")
                if t.within(TILES):
                    pool.wait_ge(xr_in[t.slot(2)], 16 * (t.turn(2) + 1))
                    settle(pool, "pool")
                    nc.gpsimd.tensor_copy(place_tok[t.slot(2)][:, :], xr[t.slot(2)][:, :, H].bitcast(I32))\
                        .then_inc(tok_copied, 1)
            steps(pool, step)

        @block.scalar
        def _(sc):
            nc_act = nc.scalar.activation

            def exps(g):
                if g.within(GRAPHS):
                    sc.wait_ge(rowmax_steps, 5 * (g.i + 1))
                    if g.past(2):
                        sc.wait_ge(probs_turned, g.i - 1)
                    for r in range(RB):
                        nc_act(e1[g.slot(2)][:, r, :], s_ps[:, r, :], ACT.Exp,
                               bias=ebias[g.slot(2)][:, 0, r:r + 1]).then_inc(exp_ready, 1)
                        nc_act(e2[g.slot(2)][:, r, :], s_ps[:, r, :], ACT.Exp,
                               bias=ebias[g.slot(2)][:, 1, r:r + 1], scale=SLOPE).then_inc(exp_ready, 1)

            def normalise(g):
                if g.within(GRAPHS):
                    sc.wait_ge(shift1_ready, g.i + 1)
                    if g.past(4):
                        sc.wait_ge(attn_ready, g.i - 3)
                    p = g.slot(2)
                    for r in range(RB):
                        nc_act(nf[g.slot(4)][:, r, 0:H], xb[g.slot(8)][:, r, :], ACT.Identity,
                               bias=shift1[p][:, r:r + 1], scale=rstd1[p][:, r:r + 1]).then_inc(nf_ready, 1)

            def copy_nfT(g):
                if g.within(GRAPHS):
                    sc.wait_ge(nfT_ready, g.i + 1)
                    if g.past(2):
                        sc.wait_ge(ad_ready, g.i - 1)
                    nc_act(nfT[g.slot(2)], nfT_ps, ACT.Copy).then_inc(nfT_copied, 1)

            def copy_probsT(g):
                if g.within(GRAPHS):
                    sc.wait_ge(probs_turned, g.i + 1)
                    if g.past(2):
                        sc.wait_ge(attn_ready, g.i - 1)
                    nc_act(probsT[g.slot(2)], probsT_ps, ACT.Copy).then_inc(probsT_ready, 1)

            def normalise2(g):
                if g.within(GRAPHS):
                    sc.wait_ge(shift2_ready, g.i + 1)
                    sc.wait_ge(rows_free, g.i + 1)
                    p = g.slot(2)
                    for r in range(RB):
                        nc_act(rowbuf[:, RB * g.slot(8) + r, 0:H], x2[g.slot(4)][:, r, :], ACT.Identity,
                               bias=shift2[p][:, r:r + 1], scale=rstd2[p][:, r:r + 1]).then_inc(xn_ready, 1)

            def copy_xnT(g):
                if g.within(GRAPHS):
                    sc.wait_ge(xnT_ready, g.i + 1)
                    if g.past(2):
                        sc.wait_ge(logits_ready, g.i - 1)
                    nc_act(xnT[g.slot(2)], xnT_ps, ACT.Copy).then_inc(xnT_copied, 1)

            def gate(b):
                sc.wait_ge(choose_steps, CHOOSE * (b + 1))
                nc_act(gate_e[:, :], gate_e[:, :], ACT.Exp).then_inc(gate_exp, 1)

            def split_hi(q):
                sc.wait_ge(w_in[q % 2], 16 * (q // 2 + 1))
                if q // 2 >= 4:
                    sc.wait_ge(plan_steps, PLAN)
                    for s in x2_stored:
                        sc.wait_ge(s, 16 * GRAPHS // 4)
                a = w_at(q // 2, 2 * (q % 2))
                nc_act(W[:, a:a + HALF], stage[q % 2][:, :], ACT.Copy, scale=WSCALE).then_inc(w_hi, 1)

            def tick(k):
                normalise2(k.back(6))
                normalise(k.back(1))
                exps(k.back(3))
                copy_probsT(k.back(4))
                copy_nfT(k.back(1))
                copy_xnT(k.back(6))
                b = k.back(11)
                if k.o % BATCH == 3 and b.within(GRAPHS):
                    gate(b.turn(BATCH))
            sc.wait_ge(const_steps, 3)
            nc_act(gate_e[:, 0:1], ones[:, 0:1], ACT.Exp).then_inc(passed["act"], 1)
            sc.wait_ge(passed["act"], 1)
            ticks(sc, tick)
            for q in range(4):
                split_hi(q)

            def x_hi(t):
                if t.within(TILES):
                    sc.wait_ge(xT_ready, t.i + 1)
                    if t.past(2):
                        sc.wait_ge(hidden_ready, 4 * (t.i - 1))
                    nc_act(xTh[t.slot(2)][:, :, :], xT_ps, ACT.Copy).then_inc(xT_hi, 1)

            def silu(t):
                if t.within(TILES):
                    e = sc.value_load(tile_expert[0:1, bass.ds(t.i, 1)], min_val=0, max_val=E - 1)
                    for j in range(4):
                        sc.wait_ge(hidden_ready, 4 * t.i + j + 1)
                        if j > 1 or t.past(1):
                            sc.wait_ge(parts_steps, 2 * (4 * t.i + j - 1))
                        settle(sc, "act")
                        for f in range(2):
                            ins = nc_act(act[j % 2][:, f, :], h_ps[j][:, f, :], ACT.Silu,
                                         bias=b1T[:, bass.ds(e * FT + 2 * j + f, 1)], scale=1.0 / WSCALE)
                        ins.then_inc(silu_ready, 1)

            def weigh(t):
                if t.within(TILES):
                    sc.wait_ge(ysum_ready, t.i + 1)
                    sc.wait_ge(weight_steps, 2 * (t.i + 1))
                    if t.past(2):
                        sc.wait_ge(added, 32 * (t.i - 1))
                    for s in range(SUB):
                        nc_act(yout[t.slot(2)][:, s, :], ysum[t.slot(2)][:, s, :], ACT.Copy,
                               scale=place_w[t.slot(2)][:, s:s + 1]).then_inc(yout_ready, 1)

            sc.wait_ge(b1_ready, 1)
            sc.wait_ge(plan_steps, PLAN)
            nc_act(gate_e[:, 0:1], ones[:, 0:1], ACT.Silu).then_inc(passed["act"], 1)
            x_hi(At(2, 0, 0))

            def step(t):
                weigh(t.back(2))
                silu(t)
                x_hi(t.back(-1))
                if isinstance(t.i, int) and t.i < E - 2:
                    split_hi(2 * (t.i + 2))
                    split_hi(2 * (t.i + 2) + 1)
            steps(sc, step)

        @block.vector
        def _(dve):
            v = nc.vector
            v.memset(template[:, :, :], 0.0).then_inc(vconst_done, 1)
            v.memset(ad_bias[:, :, :], 0.0).then_inc(vconst_done, 1)
            dve.wait_ge(vconst_done, 2)
            dve.wait_ge(vectors_in, 16 * 8)
            v.tensor_copy(ad_bias[:, :, 0], attn_b_sb[:, 0:1].to_broadcast((P, RB))).then_inc(vconst_done, 1)
            dve.wait_ge(vconst_done, 3)
            dve.wait_ge(const_steps, CONSTS)
            dve.wait_ge(b1_turned, 1)
            v.tensor_copy(b1T[:, :], b1T_ps).then_inc(b1_ready, 1)

            def stats1(g):
                if g.within(GRAPHS):
                    dve.wait_ge(x_in[g.slot(8)], 16 * (g.turn(8) + 1))
                    if g.past(1):
                        dve.wait_ge(stats1_steps, 4 * g.i)
                    for r in range(RB):
                        v.bn_stats(stat1[:, r, :], xb[g.slot(8)][:, r, :]).then_inc(stats1_steps, 1)
                    dve.wait_ge(stats1_steps, 4 * g.i + 2)
                    if g.past(2):
                        dve.wait_ge(shift1_ready, g.i - 1)
                    settle(dve, "dve")
                    for r in range(RB):
                        v.bn_aggr(mv1[g.slot(2)][:, r, :], stat1[:, r, :]).then_inc(stats1_steps, 1)

            def stats2(g):
                if g.within(GRAPHS):
                    dve.wait_ge(x2_steps, 3 * (g.i + 1))
                    if g.past(1):
                        dve.wait_ge(stats2_steps, 4 * g.i)
                    for r in range(RB):
                        v.bn_stats(stat2[:, r, :], x2[g.slot(4)][:, r, :]).then_inc(stats2_steps, 1)
                    dve.wait_ge(stats2_steps, 4 * g.i + 2)
                    if g.past(2):
                        dve.wait_ge(shift2_ready, g.i - 1)
                    settle(dve, "dve")
                    for r in range(RB):
                        v.bn_aggr(mv2[g.slot(2)][:, r, :], stat2[:, r, :]).then_inc(stats2_steps, 1)

            def shifts1(g):
                if g.within(GRAPHS):
                    dve.wait_ge(root1_steps, 2 * (g.i + 1))
                    if g.past(2):
                        dve.wait_ge(nf_ready, 2 * (g.i - 1))
                    p = g.slot(2)
                    v.scalar_tensor_tensor(out=shift1[p][:, :], in0=mv1[p][:, :, 0], scalar=-1.0, in1=rstd1[p][:, :],
                                           op0=ALU.mult, op1=ALU.mult).then_inc(shift1_ready, 1)

            def shifts2(g):
                if g.within(GRAPHS):
                    dve.wait_ge(root2_steps, 2 * (g.i + 1))
                    if g.past(2):
                        dve.wait_ge(xn_ready, 2 * (g.i - 1))
                    p = g.slot(2)
                    v.scalar_tensor_tensor(out=shift2[p][:, :], in0=mv2[p][:, :, 0], scalar=-1.0, in1=rstd2[p][:, :],
                                           op0=ALU.mult, op1=ALU.mult).then_inc(shift2_ready, 1)

            def mask(g):
                if g.within(GRAPHS):
                    dve.wait_ge(adj_in[g.slot(4)], 16 * (g.turn(4) + 1))
                    if g.past(2):
                        dve.wait_ge(scores_ready, g.i - 1)
                    v.tensor_tensor(noedge[g.slot(2)], adjb[g.slot(4)], minus_eye[:, :, :], ALU.is_equal)\
                        .then_inc(mask_ready, 1)

            def copy_ad(g):
                if g.within(GRAPHS):
                    dve.wait_ge(ad_ready, g.i + 1)
                    v.tensor_tensor(ad[g.slot(2)][:, :, :], ad_ps, ad_bias[:, :, :], ALU.add).then_inc(ad_copied, 1)

            def spread(g):
                if g.within(GRAPHS):
                    dve.wait_ge(ad_copied, g.i + 1)
                    if g.past(2):
                        dve.wait_ge(scores_ready, g.i - 1)
                    v.tensor_tensor(diag[g.slot(2)], ident[:, :].unsqueeze(1).to_broadcast((P, RB, P)),
                                    ad[g.slot(2)][:, :, 1:2].to_broadcast((P, RB, P)), ALU.mult)\
                        .then_inc(diag_ready, 1)

            def row_max(g):
                if not g.within(GRAPHS):
                    return
                n = [0]

                def link(ins):
                    n[0] += 1
                    ins.then_inc(rowmax_steps, 1)
                    dve.wait_ge(rowmax_steps, 5 * g.i + n[0])

                a = ad[g.slot(2)][:, :, 0]
                dve.wait_ge(ad_copied, g.i + 1)
                dve.wait_ge(scores_ready, g.i + 1)
                link(v.tensor_reduce(rmax[:, :], s_ps, AX.X, ALU.max))
                link(v.tensor_tensor(rz[:, :], rmax[:, :], a, ALU.add))
                link(v.scalar_tensor_tensor(out=rm[:, :], in0=rz[:, :], scalar=SLOPE, in1=rz[:, :],
                                            op0=ALU.mult, op1=ALU.max))
                if g.past(2):
                    dve.wait_ge(exp_ready, 4 * (g.i - 1))
                link(v.tensor_tensor(ebias[g.slot(2)][:, 0, :], a, rm[:, :], ALU.subtract))
                link(v.scalar_tensor_tensor(out=ebias[g.slot(2)][:, 1, :], in0=a, scalar=SLOPE, in1=rm[:, :],
                                            op0=ALU.mult, op1=ALU.subtract))

            def join(g):
                if g.within(GRAPHS):
                    dve.wait_ge(exp_ready, 4 * (g.i + 1))
                    p = g.slot(2)
                    v.tensor_tensor(e1[p], e1[p], e2[p], ALU.max).then_inc(probs_ready, 1)

            def residual(g):
                if g.within(GRAPHS):
                    dve.wait_ge(attn_ready, g.i + 1)
                    if g.past(1):
                        dve.wait_ge(x2_steps, 3 * g.i)
                    v.reciprocal(rinv[:, :], o_ps[:, :, H]).then_inc(x2_steps, 1)
                    dve.wait_ge(x2_steps, 3 * g.i + 1)
                    if g.past(4):
                        dve.wait_ge(x2_stored[g.slot(4)], 16 * g.turn(4))
                    if g.past(4):
                        dve.wait_ge(xn_ready, 2 * (g.i - 3))
                    for r in range(RB):
                        v.scalar_tensor_tensor(out=x2[g.slot(4)][:, r, :], in0=o_ps[:, r, 0:H], scalar=rinv[:, r:r + 1],
                                               in1=xb[g.slot(8)][:, r, :], op0=ALU.mult, op1=ALU.add)\
                            .then_inc(x2_steps, 1)

            def copy_logits(g):
                if g.within(GRAPHS):
                    dve.wait_ge(logits_ready, g.i + 1)
                    c = RB * g.slot(BATCH)
                    v.tensor_tensor(lg[:, c:c + RB, :], lg_ps, bg_sb[:, :, :], ALU.add).then_inc(logits_copied, 1)

            def over_experts(a):
                return a.unsqueeze(2).to_broadcast((P, COLS, E))

            def choose(b):
                n = [0]

                def link(ins):
                    n[0] += 1
                    ins.then_inc(choose_steps, 1)
                    dve.wait_ge(choose_steps, CHOOSE * b + n[0])

                dve.wait_ge(logits_copied, BATCH * (b + 1))
                link(v.tensor_reduce(top1[:, :], lg[:, :, :], AX.X, ALU.max))
                link(v.tensor_tensor(hit[:, :, :], lg[:, :, :], over_experts(top1[:, :]), ALU.is_equal))
                link(v.tensor_tensor(hit[:, :, :], hit[:, :, :], rank[:, :, :], ALU.mult))
                link(v.tensor_reduce(rank1[:, :], hit[:, :, :], AX.X, ALU.max))
                link(v.tensor_tensor(first[:, :, :], rank[:, :, :], over_experts(rank1[:, :]), ALU.is_equal))
                link(v.scalar_tensor_tensor(out=lg2[:, :, :].rearrange("p c e -> p (c e)"),
                                            in0=first[:, :, :].rearrange("p c e -> p (c e)"), scalar=-BIG,
                                            in1=lg[:, :, :].rearrange("p c e -> p (c e)"),
                                            op0=ALU.mult, op1=ALU.add))
                link(v.tensor_reduce(top2[:, :], lg2[:, :, :], AX.X, ALU.max))
                link(v.tensor_tensor(hit[:, :, :], lg2[:, :, :], over_experts(top2[:, :]), ALU.is_equal))
                link(v.tensor_tensor(hit[:, :, :], hit[:, :, :], rank[:, :, :], ALU.mult))
                link(v.tensor_reduce(rank2[:, :], hit[:, :, :], AX.X, ALU.max))
                link(v.tensor_tensor(second[:, :, :], rank[:, :, :], over_experts(rank2[:, :]), ALU.is_equal))
                link(v.tensor_tensor(sel[:, :, :], first[:, :, :], second[:, :, :], ALU.add))
                link(v.tensor_tensor(gate_e[:, :], top2[:, :], top1[:, :], ALU.subtract))
                assert n[0] == CHOOSE, n

            def place(b, half):
                n = [0]

                def link(ins):
                    n[0] += 1
                    ins.then_inc(place_steps, 1)
                    dve.wait_ge(place_steps, PLACE * b + n[0])

                mine = slice(half * COLS, (half + 1) * COLS)
                dve.wait_ge(gate_exp, b + 1)
                dve.wait_ge(prefix_ready, b + 1)
                link(v.tensor_tensor(slot_f[:, :, :], pre_ps, free_at[:, :].unsqueeze(1).to_broadcast((P, COLS, E)),
                                     ALU.add))
                link(v.tensor_tensor(free_at[:, :], tot_ps, free_at[:, :], ALU.add))
                link(v.tensor_tensor(slot_s[:, :, :], slot_f[:, :, :], first[:, :, :], ALU.mult))
                link(v.tensor_reduce(slot_1[:, mine], slot_s[:, :, :], AX.X, ALU.add))
                link(v.tensor_tensor(slot_s[:, :, :], slot_f[:, :, :], second[:, :, :], ALU.mult))
                link(v.tensor_reduce(slot_2[:, mine], slot_s[:, :, :], AX.X, ALU.add))
                link(v.tensor_copy(rowbuf[:, mine, H + 3], rank1[:, :]))
                link(v.tensor_scalar(gate_w1[:, :], gate_e[:, :], 1.0, None, ALU.add))
                link(v.reciprocal(gate_w1[:, :], gate_w1[:, :]))
                link(v.tensor_tensor(rowbuf[:, mine, H + 1], gate_e[:, :], gate_w1[:, :], ALU.mult))
                link(v.tensor_tensor(rowbuf[:, mine, H + 2], gate_w1[:, :], rowbuf[:, mine, H + 1], ALU.subtract))
                link(v.tensor_scalar(rowbuf[:, mine, H].bitcast(I32), rowbuf[:, mine, H].bitcast(I32),
                                     2 * BATCH * N, None, ALU.add))
                assert n[0] == PLACE, n

            def tick(k):
                shifts2(k.back(6))
                shifts1(k.back(1))
                row_max(k.back(3))
                copy_ad(k.back(2))
                spread(k.back(2))
                b = k.back(12)
                if k.o % BATCH == 0 and b.within(GRAPHS):
                    place(b.turn(BATCH), (b.o // BATCH) % 2)
                copy_logits(k.back(7))
                residual(k.back(5))
                stats2(k.back(5))
                stats1(k)
                mask(k.back(1))
                join(k.back(3))
                b = k.back(10)
                if k.o % BATCH == 2 and b.within(GRAPHS):
                    choose(b.turn(BATCH))
            ticks(dve, tick)

            n = [0]

            def link(ins):
                n[0] += 1
                ins.then_inc(plan_steps, 1)
                dve.wait_ge(plan_steps, n[0])

            def over_tiles(a, width):
                return a.unsqueeze(1).to_broadcast((P, TILES, width))

            link(v.tensor_copy(region_end[:, :], free_at[:, :]))
            link(v.tensor_tensor(tiles_f[:, :], free_at[:, :], coef[:, 0:E], ALU.subtract))
            link(v.tensor_scalar(cnt_i[:, :], tiles_f[:, :], float(TILE - 1), None, ALU.add))
            link(v.tensor_scalar(tiles_i[:, :], cnt_i[:, :], TILE.bit_length() - 1, None, ALU.logical_shift_right))
            link(v.tensor_scalar(tiles_f[:, :], tiles_i[:, :], 1.0, None, ALU.max))
            link(v.tensor_tensor_scan(tile_end[:, :], ones[:, 0:E], tiles_f[:, :], 0.0, ALU.mult, ALU.add))
            link(v.tensor_tensor(tiles_f[:, :], tile_end[:, :], tiles_f[:, :], ALU.subtract))
            link(v.scalar_tensor_tensor(out=coef[:, 0:E], in0=tiles_f[:, :], scalar=-float(TILE), in1=coef[:, 0:E],
                                        op0=ALU.mult, op1=ALU.add))
            link(v.memset(coef[:, E:E + 1], 1e6))
            link(v.tensor_tensor(past[:, :, 0:E], over_tiles(tile_end[:, :], E),
                                 tile_no[:, :].unsqueeze(2).to_broadcast((P, TILES, E)), ALU.is_le))
            link(v.tensor_reduce(tile_e[:, :], past[:, :, 0:E], AX.X, ALU.add))
            link(v.tensor_scalar(tile_rank[:, :], tile_e[:, :], -1.0, float(E), ALU.mult, ALU.add))
            link(v.tensor_scalar(tile_expert[:, :], tile_e[:, :], float(E - 1), None, ALU.min))
            link(v.tensor_tensor(past[:, :, :], over_tiles(expert_no[:, :], E + 1),
                                 tile_e[:, :].unsqueeze(2).to_broadcast((P, TILES, E + 1)), ALU.is_equal))
            link(v.tensor_tensor(past[:, :, :], past[:, :, :], over_tiles(coef[:, :], E + 1), ALU.mult))
            link(v.tensor_reduce(tile_b[:, :], past[:, :, :], AX.X, ALU.add))
            link(v.scalar_tensor_tensor(out=tile_b[:, :], in0=tile_no[:, :], scalar=float(TILE), in1=tile_b[:, :],
                                        op0=ALU.mult, op1=ALU.add))
            link(v.tensor_scalar(tile_base[:, :], tile_b[:, :], float(NULL_BASE), None, ALU.min))
            assert n[0] == PLAN, n

            def split_lo(q):
                dve.wait_ge(w_hi, q + 1)
                a = w_at(q // 2, 2 * (q % 2))
                v.scalar_tensor_tensor(out=W[:, a + HALF:a + 2 * HALF], in0=stage[q % 2][:, :], scalar=WSCALE,
                                       in1=W[:, a:a + HALF], op0=ALU.mult, op1=ALU.subtract).then_inc(w_lo, 1)

            for q in range(4):
                split_lo(q)

            def x_lo(t):
                if t.within(TILES):
                    dve.wait_ge(xT_hi, t.i + 1)
                    v.tensor_tensor(xTl[t.slot(2)][:, :, :], xT_ps, xTh[t.slot(2)][:, :, :], ALU.subtract)\
                        .then_inc(xT_lo, 1)

            def parts(t):
                if t.within(TILES):
                    hi, lo = hid[t.slot(2)]
                    if t.past(2):
                        dve.wait_ge(y_ready, t.i - 1)
                    for j in range(4):
                        dve.wait_ge(silu_ready, 4 * t.i + j + 1)
                        pair = slice(2 * j, 2 * j + 2)
                        v.tensor_copy(hi[:, pair, :], act[j % 2][:, :, :]).then_inc(parts_steps, 1)
                        dve.wait_ge(parts_steps, 2 * (4 * t.i + j) + 1)
                        v.tensor_tensor(lo[:, pair, :], act[j % 2][:, :, :], hi[:, pair, :], ALU.subtract)\
                            .then_inc(parts_steps, 1)

            def sum_up(t):
                if t.within(TILES):
                    e = dve.value_load(tile_expert[0:1, bass.ds(t.i, 1)], min_val=0, max_val=E - 1)
                    dve.wait_ge(y_ready, t.i + 1)
                    if t.past(2):
                        dve.wait_ge(yout_ready, 2 * (t.i - 1))
                    v.scalar_tensor_tensor(out=ysum[t.slot(2)][:, :, :], in0=y_ps[t.slot(2)], scalar=1.0 / WSCALE,
                                           in1=b2_sb[:, bass.ds(e, 1), :].to_broadcast((P, SUB, H)),
                                           op0=ALU.mult, op1=ALU.add).then_inc(ysum_ready, 1)

            def weights(t):
                if t.within(TILES):
                    r = xr[t.slot(2)]
                    dve.wait_ge(xr_in[t.slot(2)], 16 * (t.turn(2) + 1))
                    if t.past(1):
                        dve.wait_ge(weight_steps, 2 * t.i)
                    v.scalar_tensor_tensor(out=place_q[:, :], in0=r[:, :, H + 3], scalar=tile_rank[:, bass.ds(t.i, 1)],
                                           in1=r[:, :, H + 2], op0=ALU.is_equal, op1=ALU.mult)\
                        .then_inc(weight_steps, 1)
                    dve.wait_ge(weight_steps, 2 * t.i + 1)
                    if t.past(2):
                        dve.wait_ge(yout_ready, 2 * (t.i - 1))
                    v.tensor_tensor(place_w[t.slot(2)][:, :], place_q[:, :], r[:, :, H + 1], ALU.add)\
                        .then_inc(weight_steps, 1)

            x_lo(At(2, 0, 0))

            def step(t):
                sum_up(t.back(2))
                parts(t)
                x_lo(t.back(-1))
                weights(t)
                if isinstance(t.i, int) and t.i < E - 2:
                    split_lo(2 * (t.i + 2))
                    split_lo(2 * (t.i + 2) + 1)
            steps(dve, step)

        @block.tensor
        def _(pe):
            mm, tp = nc.tensor.matmul, nc.tensor.transpose
            pe.wait_ge(const_steps, CONSTS)
            pe.wait_ge(vectors_in, 16 * 8)
            tp(b1T_ps, b1_rows[:, :], ident[0:E * FT, 0:E * FT]).then_inc(b1_turned, 1)

            def turn_nf(g):
                if g.within(GRAPHS):
                    pe.wait_ge(nf_ready, 2 * (g.i + 1))
                    if g.past(1):
                        pe.wait_ge(nfT_copied, g.i)
                    for r in range(RB):
                        for k in range(KT):
                            ins = tp(nfT_ps[:, k, r * P:(r + 1) * P], nf[g.slot(4)][:, r, k * P:(k + 1) * P],
                                     ident[:, :])
                    ins.then_inc(nfT_ready, 1)

            def attend(g):
                if g.within(GRAPHS):
                    pe.wait_ge(probsT_ready, g.i + 1)
                    if g.past(1):
                        pe.wait_ge(x2_steps, 3 * g.i)
                    for r in range(RB):
                        for j in range(RB):
                            ins = mm(o_ps[:, r, 0:H + 1], probsT[g.slot(2)][:, j, r * P:(r + 1) * P],
                                     nf[g.slot(4)][:, j, 0:H + 1], start=(j == 0), stop=(j == RB - 1))
                    ins.then_inc(attn_ready, 1)

            def node_scores(g):
                if g.within(GRAPHS):
                    pe.wait_ge(nfT_copied, g.i + 1)
                    if g.past(1):
                        pe.wait_ge(ad_copied, g.i)
                    for r in range(RB):
                        for k in range(KT):
                            ins = mm(ad_ps[:, r, :], nfT[g.slot(2)][:, k, r * P:(r + 1) * P], w_sd[:, k, :],
                                     start=(k == 0), stop=(k == KT - 1))
                    ins.then_inc(ad_ready, 1)

            def edge_scores(g):
                if g.within(GRAPHS):
                    pe.wait_ge(diag_ready, g.i + 1)
                    pe.wait_ge(mask_ready, g.i + 1)
                    if g.past(1):
                        pe.wait_ge(exp_ready, 4 * g.i)
                    for j in range(RB):
                        mm(s_ps[:, :, j * P:(j + 1) * P], ones[:, :],
                           diag[g.slot(2)][:, j, :].unsqueeze(1).to_broadcast((P, RB, P)), start=(j == 0), stop=False)
                    mm(s_ps, minus_big[:, :], noedge[g.slot(2)], start=False, stop=True).then_inc(scores_ready, 1)

            def turn_probs(g):
                if g.within(GRAPHS):
                    pe.wait_ge(probs_ready, g.i + 1)
                    if g.past(1):
                        pe.wait_ge(probsT_ready, g.i)
                    for r in range(RB):
                        for j in range(RB):
                            ins = tp(probsT_ps[:, j, r * P:(r + 1) * P], e1[g.slot(2)][:, r, j * P:(j + 1) * P],
                                     ident[:, :])
                    ins.then_inc(probs_turned, 1)

            def turn_xn(g):
                if g.within(GRAPHS):
                    pe.wait_ge(xn_ready, 2 * (g.i + 1))
                    if g.past(1):
                        pe.wait_ge(xnT_copied, g.i)
                    for r in range(RB):
                        for k in range(KT):
                            ins = tp(xnT_ps[:, k, r * P:(r + 1) * P],
                                     rowbuf[:, RB * g.slot(8) + r, k * P:(k + 1) * P], ident[:, :])
                    ins.then_inc(xnT_ready, 1)

            def gate_logits(g):
                if g.within(GRAPHS):
                    pe.wait_ge(xnT_copied, g.i + 1)
                    if g.past(1):
                        pe.wait_ge(logits_copied, g.i)
                    if g.o % BATCH == 1 and g.past(4):
                        pe.wait_ge(place_steps, PLACE * g.turn(BATCH))
                    for r in range(RB):
                        for k in range(KT):
                            ins = mm(lg_ps[:, r, :], xnT[g.slot(2)][:, k, r * P:(r + 1) * P], wg_sb[:, k, :],
                                     start=(k == 0), stop=(k == KT - 1))
                    ins.then_inc(logits_ready, 1)

            def count(b):
                pe.wait_ge(logits_copied, capped(BATCH * b + BATCH + 1, GRAPHS))
                pe.wait_ge(choose_steps, CHOOSE * b + 12)
                mm(pre_ps, before[:, :], sel[:, :, :], start=True, stop=False)
                for c in range(COLS - 1):
                    mm(pre_ps[:, c + 1:COLS, :], ones_bf[:, :],
                       sel[:, c:c + 1, :].to_broadcast((P, COLS - 1 - c, E)), start=False, stop=(c == COLS - 2))
                for c in range(COLS):
                    ins = mm(tot_ps, ones_bf[:, :], sel[:, c, :], start=(c == 0), stop=(c == COLS - 1))
                ins.then_inc(prefix_ready, 1)

            def tick(k):
                attend(k.back(5))
                node_scores(k.back(2))
                gate_logits(k.back(7))
                turn_probs(k.back(4))
                turn_nf(k.back(1))
                turn_xn(k.back(6))
                edge_scores(k.back(2))
                b = k.back(11)
                if k.o % BATCH == 3 and b.within(GRAPHS):
                    count(b.turn(BATCH))
            ticks(pe, tick)

            def turn_x(t):
                if t.within(TILES):
                    pe.wait_ge(xr_in[t.slot(2)], 16 * (t.turn(2) + 1))
                    if t.past(1):
                        pe.wait_ge(xT_lo, t.i)
                    for s in range(SUB):
                        for k in range(KT):
                            ins = tp(xT_ps[:, k, s * P:(s + 1) * P], xr[t.slot(2)][:, s, k * P:(k + 1) * P],
                                     ident[:, :])
                    ins.then_inc(xT_ready, 1)

            def hidden(t):
                if t.within(TILES):
                    e = pe.value_load(tile_expert[0:1, bass.ds(t.i, 1)], min_val=0, max_val=E - 1)
                    pe.wait_ge(xT_lo, t.i + 1)
                    if isinstance(t.i, int) and t.i < E:
                        pe.wait_ge(w_lo, 2 * (t.i + 1))
                    for j in range(4):
                        if t.past(1):
                            pe.wait_ge(silu_ready, 4 * (t.i - 1) + j + 1)
                        settle(pe, "pe")
                        for f in (2 * j, 2 * j + 1):
                            n = 0
                            for k in range(KT):
                                for part, xT in ((0, xTh), (0, xTl), (1, xTh)):
                                    at = (part * HALF + k * FF + f * P)
                                    ins = mm(h_ps[j][:, f % 2, :], W[:, bass.ds(e * (4 * HALF) + at, P)],
                                             xT[t.slot(2)][:, k, :], start=(n == 0), stop=(n == 5))
                                    n += 1
                        ins.then_inc(hidden_ready, 1)

            def result(t):
                if t.within(TILES):
                    e = pe.value_load(tile_expert[0:1, bass.ds(t.i, 1)], min_val=0, max_val=E - 1)
                    hi, lo = hid[t.slot(2)]
                    pe.wait_ge(parts_steps, 8 * (t.i + 1))
                    if t.past(2):
                        pe.wait_ge(ysum_ready, t.i - 1)
                    for s in range(SUB):
                        n = 0
                        for f in range(FT):
                            for src, part in ((hi, 2), (lo, 2), (hi, 3)):
                                at = part * HALF + f * H
                                ins = mm(y_ps[t.slot(2)][:, s, :], src[:, f, s * P:(s + 1) * P],
                                         W[:, bass.ds(e * (4 * HALF) + at, H)], start=(n == 0), stop=(n == 3 * FT - 1))
                                n += 1
                    ins.then_inc(y_ready, 1)

            pe.wait_ge(plan_steps, PLAN)
            turn_x(At(2, 0, 0))

            def step(t):
                hidden(t)
                turn_x(t.back(-1))
                result(t.back(1))
            steps(pe, step)


_INS = ["x", "adj", "L0_gnn_attn_w_src", "L0_gnn_attn_w_dst", "L0_gnn_attn_b", "L0_ffn_Wg", "L0_ffn_bg",
        "L0_ffn_W1", "L0_ffn_b1", "L0_ffn_W2", "L0_ffn_b2"]


def kernel(**inputs):
    import numpy as _np
    import concourse.bacc as _bacc
    from concourse import mybir as _mybir
    from concourse.bass_utils import run_bass_kernel_spmd as _run

    nc = _bacc.Bacc("TRN2", target_bir_lowering=False, num_devices=1)
    arrays, args = {}, []
    for name in _INS:
        a = _np.ascontiguousarray(inputs[name])
        arrays[f"in_{name}_dram"] = a
        args.append(nc.dram_tensor(f"in_{name}_dram", a.shape, _mybir.dt.from_np(a.dtype), kind="ExternalInput").ap())
    out = nc.dram_tensor("out_0_dram", (TOKENS + TRASH, H), F32, kind="ExternalOutput").ap()
    build_gat_moe(nc, *args, out)
    r = _run(nc, [arrays], core_ids=[0])
    return r.results[0]["out_0_dram"][:TOKENS].reshape(GRAPHS, N, H)
```

```python
from contextlib import ExitStack

import concourse.bass as bass
from concourse import mybir

F32 = mybir.dt.float32
F16 = mybir.dt.float16
BF16 = mybir.dt.bfloat16
I32 = mybir.dt.int32
ALU = mybir.AluOpType
ACT = mybir.ActivationFunctionType
AX = mybir.AxisListType

P = 128
GRAPHS = 32
N = 256
H = 256
E = 8
FF = 1024
RB = N // P
KT = H // P
FT = FF // P
TOKENS = GRAPHS * N
TRASH = P
TILE = 256
SUB = TILE // P
TILES = (2 * TOKENS) // TILE + E - 1
REGION = TOKENS + TILE
NULL_BASE = E * REGION
WORDS = H + 4
EPS = 1e-5
SLOPE = 0.2
BIG = 1e30
WSCALE = 256.0
U = 8
BATCH = 4
COLS = BATCH * RB
HALF = KT * FF
STAGES = 46


class At:

    def __init__(self, unit, m, o):
        self.unit, self.m, self.o = unit, m, o
        self.i = unit * m + o

    def back(self, n):
        return At(self.unit, self.m, self.o - n)

    def slot(self, n):
        return self.o % n

    def turn(self, n):
        return (self.unit // n) * self.m + self.o // n

    def within(self, n):
        return not isinstance(self.i, int) or 0 <= self.i < n

    def past(self, n):
        return not isinstance(self.i, int) or self.i >= n


def capped(value, n):
    return min(value, n) if isinstance(value, int) else value


def build_gat_moe(nc, x, adj, w_src, w_dst, attn_b, w_gate, b_gate, w1, b1, w2, b2, out):
    rows = nc.dram_tensor("expert_rows", [NULL_BASE + TILE, WORDS], F32, kind="Internal").ap()
    x_rows = x.rearrange("g (r p) h -> g p r h", p=P)
    adj_rows = adj.rearrange("g (r p) n -> g p r n", p=P)
    out_rows = out[0:TOKENS, :].rearrange("(g r p) h -> g p r h", r=RB, p=P)
    w1_rows = w1.rearrange("e (k p) f -> e p k f", p=P)
    w2_rows = w2.rearrange("e (t p) h -> e p t h", p=P)

    ctx = ExitStack()
    with ctx:
        def sb(name, shape, dt):
            return ctx.enter_context(nc.sbuf_tensor(name, shape, dt))[tuple(slice(0, n) for n in shape)]

        def sem(name):
            return ctx.enter_context(nc.semaphore(name))

        ctx.enter_context(nc.allow_non_contiguous_dma(reason="a few small vectors"))
        ctx.enter_context(nc.allow_low_precision(reason="places are whole numbers below 2^24"))

        W = sb("W", [P, E * 4 * HALF], F16)
        arena_at = [4 * 4 * HALF]

        def arena(words, dt=F32):
            a = arena_at[0]
            arena_at[0] += 2 * words
            assert arena_at[0] <= E * 4 * HALF
            v = W[:, a:a + 2 * words]
            return v if dt == F16 else v.bitcast(dt)

        xb = [arena(RB * H).rearrange("p (r h) -> p r h", r=RB) for _ in range(8)]
        adjb = [arena(RB * N, I32).rearrange("p (r n) -> p r n", r=RB) for _ in range(4)]
        nf = [arena(RB * (H + 2)).rearrange("p (r h) -> p r h", r=RB) for _ in range(4)]
        nfT = [arena(KT * N).rearrange("p (k n) -> p k n", k=KT) for _ in range(2)]
        noedge = [arena(RB * N // 2, BF16).rearrange("p (r n) -> p r n", r=RB) for _ in range(2)]
        diag = [arena(RB * P).rearrange("p (j n) -> p j n", j=RB) for _ in range(2)]
        e1_both = arena(2 * RB * N)
        e1 = [e1_both[:, i * RB * N:(i + 1) * RB * N].rearrange("p (r n) -> p r n", r=RB) for i in range(2)]
        e2 = [arena(RB * N).rearrange("p (r n) -> p r n", r=RB) for _ in range(2)]
        probsT = [arena(RB * N).rearrange("p (j n) -> p j n", j=RB) for _ in range(2)]
        x2 = [arena(RB * H).rearrange("p (r h) -> p r h", r=RB) for _ in range(2)]

        xnT = [arena(KT * N).rearrange("p (k n) -> p k n", k=KT) for _ in range(2)]

        row_region = sb("row_region", [P, 2 * COLS * WORDS], F32)
        rowbuf = row_region[:, :].rearrange("p (c w) -> p c w", w=WORDS)
        x2 += [sb(f"x2_{i}", [P, RB, H], F32) for i in range(2)]
        stage = [sb(f"stage{i}", [P, HALF], F32) for i in range(2)]

        hparts = row_region[:, 0:2 * 2 * FT * TILE // 2].bitcast(F16)\
            .rearrange("p (b q f n) -> p b q f n", b=2, q=2, f=FT)
        hid = [[hparts[:, b, q, :, :] for q in range(2)] for b in range(2)]
        xr = [sb(f"xr{i}", [P, SUB, WORDS], F32) for i in range(2)]
        xTh = [sb(f"xTh{i}", [P, KT, TILE], F16) for i in range(2)]
        xTl = [sb(f"xTl{i}", [P, KT, TILE], F16) for i in range(2)]
        act = [sb(f"act{i}", [P, 2, TILE], F32) for i in range(2)]
        ysum = [sb(f"ysum{i}", [P, SUB, H], F32) for i in range(2)]
        yout = [sb(f"yout{i}", [P, SUB, H], F32) for i in range(2)]
        place_tok = [sb(f"place_tok{i}", [P, SUB], I32) for i in range(2)]
        place_w = [sb(f"place_w{i}", [P, SUB], F32) for i in range(2)]
        place_q = sb("place_q", [P, SUB], F32)

        ident = sb("ident", [P, P], F32)
        ones = sb("ones", [P, P], F32)
        eps = sb("eps", [P, RB], F32)
        minus_half = sb("minus_half", [P, RB], F32)
        ones_bf = sb("ones_bf", [P, P], BF16)
        minus_big = sb("minus_big", [P, P], BF16)
        before = sb("before", [P, P], BF16)
        minus_eye = sb("minus_eye", [P, RB, N], F32)
        rank = sb("rank", [P, COLS, E], F32)
        expert_no = sb("expert_no", [P, E + 1], F32)
        tile_no = sb("tile_no", [P, TILES], F32)
        template = sb("template", [P, SUB, WORDS], F32)
        w_sd = sb("w_sd", [P, KT, 2], F32)
        wg_sb = sb("wg_sb", [P, KT, E], F32)
        bg_sb = sb("bg_sb", [P, RB, E], F32)
        attn_b_sb = sb("attn_b_sb", [P, 1], F32)
        ad_bias = sb("ad_bias", [P, RB, 2], F32)
        b1_rows = sb("b1_rows", [E * FT, P], F32)
        b1T = sb("b1T", [P, E * FT], F32)
        b2_sb = sb("b2_sb", [P, E, H], F32)

        stat1 = sb("stat1", [P, RB, 6], F32)
        stat2 = sb("stat2", [P, RB, 6], F32)
        mv1 = [sb(f"mv1_{i}", [P, RB, 2], F32) for i in range(2)]
        mv2 = [sb(f"mv2_{i}", [P, RB, 2], F32) for i in range(2)]
        var1 = sb("var1", [P, RB], F32)
        var2 = sb("var2", [P, RB], F32)
        rstd1 = [sb(f"rstd1_{i}", [P, RB], F32) for i in range(2)]
        rstd2 = [sb(f"rstd2_{i}", [P, RB], F32) for i in range(2)]
        shift1 = [sb(f"shift1_{i}", [P, RB], F32) for i in range(2)]
        shift2 = [sb(f"shift2_{i}", [P, RB], F32) for i in range(2)]
        ad = [sb(f"ad{i}", [P, RB, 2], F32) for i in range(2)]
        rmax = sb("rmax", [P, RB], F32)
        rz = sb("rz", [P, RB], F32)
        rm = sb("rm", [P, RB], F32)
        ebias = [sb(f"ebias{i}", [P, 2, RB], F32) for i in range(2)]
        rinv = sb("rinv", [P, RB], F32)
        lg = sb("lg", [P, COLS, E], F32)
        lg2 = sb("lg2", [P, COLS, E], F32)
        hit = sb("hit", [P, COLS, E], F32)
        first = sb("first", [P, COLS, E], F32)
        second = sb("second", [P, COLS, E], F32)
        top1 = sb("top1", [P, COLS], F32)
        top2 = sb("top2", [P, COLS], F32)
        rank1 = sb("rank1", [P, COLS], F32)
        rank2 = sb("rank2", [P, COLS], F32)
        sel = sb("sel", [P, COLS, E], BF16)
        gate_e = sb("gate_e", [P, COLS], F32)
        gate_w1 = sb("gate_w1", [P, COLS], F32)
        slot_f = sb("slot_f", [P, COLS, E], F32)
        slot_s = [sb(f"slot_s{i}", [P, COLS, E], F32) for i in range(2)]
        slot_1 = sb("slot_1", [P, 2 * COLS], I32)
        slot_2 = sb("slot_2", [P, 2 * COLS], I32)
        free_at = sb("free_at", [P, E], F32)
        cnt_i = sb("cnt_i", [P, E], I32)
        tiles_i = sb("tiles_i", [P, E], I32)
        tiles_f = sb("tiles_f", [P, E], F32)
        tile_end = sb("tile_end", [P, E], F32)
        coef = sb("coef", [P, E + 1], F32)
        past = e1_both[:, 0:TILES * (E + 1)].rearrange("p (t e) -> p t e", e=E + 1)
        tile_e = sb("tile_e", [P, TILES], F32)
        tile_rank = sb("tile_rank", [P, TILES], F32)
        tile_b = sb("tile_b", [P, TILES], F32)
        region_end = sb("region_end", [P, E], I32)
        tile_expert = sb("tile_expert", [P, TILES], I32)
        tile_base = sb("tile_base", [P, TILES], I32)

        bank = [ctx.enter_context(nc.psum_tensor(f"bank{i}", [P, 512], F32)) for i in range(4)]
        o_ps = ctx.enter_context(nc.psum_tensor("o_ps", [P, RB, 512], F32))
        bank += [None, None] + [ctx.enter_context(nc.psum_tensor(f"bank{i}", [P, 512], F32)) for i in (6, 7)]
        nfT_ps = bank[0][:, :].rearrange("p (k n) -> p k n", k=KT)
        s_ps = bank[1][:, :].rearrange("p (r n) -> p r n", r=RB)
        probsT_ps = bank[2][:, :].rearrange("p (j n) -> p j n", j=RB)
        xnT_ps = bank[6][:, :].rearrange("p (k n) -> p k n", k=KT)
        small = bank[7]
        ad_ps = small[:, 0:RB * 2].rearrange("p (r a) -> p r a", r=RB)
        lg_ps = small[:, 16:16 + RB * E].rearrange("p (r e) -> p r e", r=RB)
        pre_ps = bank[3][:, 64:64 + COLS * E].rearrange("p (c e) -> p c e", c=COLS)
        tot_ps = bank[3][:, 128:128 + E]
        b1T_ps = small[:, 256:256 + E * FT]
        xT_ps = bank[0][:, :].rearrange("p (k n) -> p k n", k=KT)
        h_ps = [bank[1], bank[2], bank[3], bank[6]]
        h_ps = [b[:, :].rearrange("p (f n) -> p f n", f=2) for b in h_ps]
        y_ps = [o_ps[:, i, :].rearrange("p (s h) -> p s h", s=SUB) for i in range(2)]

        x_in = [sem(f"x_in{i}") for i in range(8)]
        adj_in = [sem(f"adj_in{i}") for i in range(4)]
        x2_stored = [sem(f"x2_stored{i}") for i in range(4)]
        scatter_done = [sem(f"scatter_done{i}") for i in range(8)]
        vectors_in = sem("vectors_in")
        const_steps = sem("const_steps")
        vconst_done = sem("vconst_done")
        trash_zeroed = sem("trash_zeroed")
        b1_turned = sem("b1_turned")
        b1_ready = sem("b1_ready")
        stats1_steps = sem("stats1_steps")
        stats2_steps = sem("stats2_steps")
        root1_steps = sem("root1_steps")
        root2_steps = sem("root2_steps")
        shift1_ready = sem("shift1_ready")
        shift2_ready = sem("shift2_ready")
        nf_ready = sem("nf_ready")
        nfT_ready = sem("nfT_ready")
        nfT_copied = sem("nfT_copied")
        ad_ready = sem("ad_ready")
        ad_copied = sem("ad_copied")
        diag_ready = sem("diag_ready")
        mask_ready = sem("mask_ready")
        scores_ready = sem("scores_ready")
        rowmax_steps = sem("rowmax_steps")
        exp_ready = sem("exp_ready")
        probs_ready = sem("probs_ready")
        probs_turned = sem("probs_turned")
        probsT_ready = sem("probsT_ready")
        attn_ready = sem("attn_ready")
        x2_steps = sem("x2_steps")
        xn_ready = sem("xn_ready")
        xnT_ready = sem("xnT_ready")
        xnT_copied = sem("xnT_copied")
        logits_ready = sem("logits_ready")
        logits_copied = sem("logits_copied")
        choose_steps = sem("choose_steps")
        prefix_ready = sem("prefix_ready")
        gate_exp = sem("gate_exp")
        rows_free = sem("rows_free")
        place_steps = sem("place_steps")
        plan_steps = sem("plan_steps")
        padded = sem("padded")
        w_in = [sem(f"w_in{i}") for i in range(2)]
        w_hi = sem("w_hi")
        w_lo = sem("w_lo")
        xr_in = [sem(f"xr_in{i}") for i in range(2)]
        xT_ready = sem("xT_ready")
        xT_hi = sem("xT_hi")
        xT_lo = sem("xT_lo")
        hidden_ready = sem("hidden_ready")
        silu_ready = sem("silu_ready")
        parts_steps = sem("parts_steps")
        y_ready = sem("y_ready")
        ysum_ready = sem("ysum_ready")
        weight_steps = sem("weight_steps")
        yout_ready = sem("yout_ready")
        tok_copied = sem("tok_copied")
        added = sem("added")
        passed = {k: sem(f"passed_{k}") for k in ("pe", "act", "dve", "pool", "sp")}

        def settle(eng, who):
            eng.sem_inc(passed[who], 1)

        DRAIN_SPLITS = 3
        SPLIT_TICKS = [36, 38, 41]
        STEP_SPLITS = [(6,), (7,), (8,), (9, 10), (11,), (12, 13), (14,), (15,)]
        assert STEP_SPLITS[-1][-1] == 2 * E - 1
        CONSTS = 23
        CHOOSE = 13
        PLACE = 12
        PLAN = 18

        def ticks(eng, tick):
            for k in range(2 * U):
                tick(At(U, k // U, k % U))
            with eng.Fori(2, GRAPHS // U) as m:
                for k in range(U):
                    tick(At(U, m, k))
            for k in range(GRAPHS, STAGES):
                tick(At(U, k // U, k % U))

        SPLIT_STEPS = E + 1
        TURNS = (TILES - SPLIT_STEPS) // 2 - 1
        assert SPLIT_STEPS + 2 * TURNS + 2 == TILES

        def steps(eng, step):
            for t in range(SPLIT_STEPS):
                step(At(2, 0, t))
            with eng.Fori(0, TURNS) as m:
                for o in range(2):
                    step(At(2, m, SPLIT_STEPS + o))
            for t in range(TILES - 2, TILES + 2):
                step(At(2, 0, t))

        def w_at(e, part):
            return (e * 4 + part) * HALF

        block = ctx.enter_context(nc.Block())

        @block.sync
        def _(sp):
            def load_x(g):
                if g.within(GRAPHS):
                    if g.past(8):
                        sp.wait_ge(x2_steps, 3 * (g.i - 7))
                    settle(sp, "sp")
                    sp.dma_start(xb[g.slot(8)], x_rows[bass.ds(g.i, 1)].rearrange("g p r h -> (g p) r h"))\
                        .then_inc(x_in[g.slot(8)], 16)

            def load_adj(g):
                if g.within(GRAPHS):
                    if g.past(4):
                        sp.wait_ge(mask_ready, g.i - 3)
                    settle(sp, "sp")
                    sp.dma_start(adjb[g.slot(4)], adj_rows[bass.ds(g.i, 1)].rearrange("g p r n -> (g p) r n"))\
                        .then_inc(adj_in[g.slot(4)], 16)

            def store_x2(g):
                if g.within(GRAPHS):
                    sp.wait_ge(x2_steps, 3 * (g.i + 1))
                    settle(sp, "sp")
                    sp.dma_start(out_rows[bass.ds(g.i, 1)].rearrange("g p r h -> (g p) r h"), x2[g.slot(4)])\
                        .then_inc(x2_stored[g.slot(4)], 16)

            def load_w(q):
                if q >= 2:
                    sp.wait_ge(w_lo, q - 1)
                src = w1_rows if q % 2 == 0 else w2_rows
                sp.dma_start(stage[q % 2][:, :].rearrange("p (k f) -> p k f", k=KT if q % 2 == 0 else FT),
                             src[q // 2]).then_inc(w_in[q % 2], 16)

            load_x(At(U, 0, 0))
            load_adj(At(U, 0, 0))
            sp.dma_start(w_sd[:, :, 0], w_src.rearrange("(k p) -> p k", p=P)).then_inc(vectors_in, 16)
            sp.dma_start(w_sd[:, :, 1], w_dst.rearrange("(k p) -> p k", p=P)).then_inc(vectors_in, 16)
            sp.dma_start(attn_b_sb[:, :], attn_b.rearrange("(a n) -> a n", a=1).to_broadcast((P, 1)))\
                .then_inc(vectors_in, 16)
            sp.dma_start(wg_sb[:, :, :], w_gate.rearrange("(k p) e -> p k e", p=P)).then_inc(vectors_in, 16)
            for r in range(RB):
                sp.dma_start(bg_sb[:, r, :], b_gate.rearrange("(a n) -> a n", a=1).to_broadcast((P, E)))\
                    .then_inc(vectors_in, 16)
            sp.dma_start(b1_rows[:, :], b1.rearrange("e (t p) -> (e t) p", p=P)).then_inc(vectors_in, 16)
            sp.dma_start(b2_sb[:, :, :].rearrange("p e h -> p (e h)"),
                         b2.rearrange("(a e) h -> a (e h)", a=1).to_broadcast((P, E * H))).then_inc(vectors_in, 16)

            def tick(k):
                store_x2(k.back(9))
                if not (isinstance(k.i, int) and k.i == 1):
                    load_adj(k.back(1))
                if not (isinstance(k.i, int) and k.i == 0):
                    load_x(k)
                if isinstance(k.i, int) and k.i == U - 1:
                    load_w(0)
                    load_w(1)
                    sp.wait_ge(vconst_done, 1)
                    sp.dma_start(out[TOKENS:TOKENS + TRASH, :], template[:, 0, 0:H]).then_inc(trash_zeroed, 16)
                if isinstance(k.i, int) and k.i == GRAPHS + 2:
                    sp.wait_ge(const_steps, CONSTS)
                    sp.dma_start(rows[NULL_BASE:NULL_BASE + TILE, :].rearrange("(s p) w -> p s w", p=P),
                                 template[:, :, :]).then_inc(padded, 16)
            ticks(sp, tick)
            for q in range(2, DRAIN_SPLITS + 2):
                load_w(q)
            sp.wait_ge(plan_steps, PLAN)
            for e in range(E):
                end = sp.value_load(region_end[0:1, e:e + 1], min_val=e * REGION, max_val=e * REGION + TOKENS)
                sp.dma_start(rows[bass.ds(end, TILE), :].rearrange("(s p) w -> p s w", p=P),
                             template[:, :, :]).then_inc(padded, 16)
            for q in range(DRAIN_SPLITS + 2, STEP_SPLITS[0][0]):
                load_w(q)
            sp.wait_ge(padded, 16 * (E + 1))
            for s in scatter_done:
                sp.wait_ge(s, 64 * GRAPHS // 8)

            def step(t):
                if t.within(TILES):
                    base = sp.value_load(tile_base[0:1, bass.ds(t.i, 1)], min_val=0, max_val=NULL_BASE)
                    if t.past(2):
                        sp.wait_ge(weight_steps, 2 * (t.i - 1))
                    if t.past(2):
                        sp.wait_ge(xT_ready, t.i - 1)
                    if t.past(2):
                        sp.wait_ge(tok_copied, t.i - 1)
                    settle(sp, "sp")
                    sp.dma_start(xr[t.slot(2)][:, :, :],
                                 rows[bass.ds(base, TILE), :].rearrange("(s p) w -> p s w", p=P))\
                        .then_inc(xr_in[t.slot(2)], 16)
                if isinstance(t.i, int) and t.i < len(STEP_SPLITS):
                    for q in STEP_SPLITS[t.i]:
                        load_w(q)
            steps(sp, step)

        @block.gpsimd
        def _(pool):
            done = [0]

            def const(ins):
                done[0] += 1
                ins.then_inc(const_steps, 1)
                pool.wait_ge(const_steps, done[0])

            const(nc.gpsimd.memset(ident[:, :], 0.0))
            const(nc.gpsimd.affine_select(out=ident[:, :], in_=ident[:, :], compare_op=ALU.not_equal, fill=1.0,
                                          base=0, pattern=[[-1, P]], channel_multiplier=1))
            const(nc.gpsimd.memset(ones[:, :], 1.0))
            const(nc.gpsimd.memset(eps[:, :], EPS))
            const(nc.gpsimd.memset(minus_half[:, :], -0.5))
            const(nc.gpsimd.memset(minus_eye[:, :, :], 0.0))
            const(nc.gpsimd.affine_select(out=minus_eye[:, :, :], in_=minus_eye[:, :, :], compare_op=ALU.not_equal,
                                          fill=-1.0, base=0, pattern=[[P, RB], [-1, N]], channel_multiplier=1))
            for i in range(4):
                const(nc.gpsimd.memset(nf[i][:, :, H:H + 1], 1.0))
            const(nc.gpsimd.memset(ones_bf[:, :], 1.0))
            const(nc.gpsimd.memset(minus_big[:, :], 0.0))
            const(nc.gpsimd.affine_select(out=minus_big[:, :], in_=minus_big[:, :], compare_op=ALU.not_equal,
                                          fill=-BIG, base=0, pattern=[[-1, P]], channel_multiplier=1))
            const(nc.gpsimd.affine_select(out=before[:, :], in_=ones_bf[:, :], compare_op=ALU.is_gt, fill=0.0,
                                          base=0, pattern=[[1, P]], channel_multiplier=-1))
            const(nc.gpsimd.iota(rank[:, :, :], pattern=[[0, COLS], [-1, E]], base=E, channel_multiplier=0,
                                 allow_small_or_imprecise_dtypes=True))
            const(nc.gpsimd.iota(expert_no[:, :], pattern=[[1, E + 1]], base=0, channel_multiplier=0,
                                 allow_small_or_imprecise_dtypes=True))
            const(nc.gpsimd.iota(tile_no[:, :], pattern=[[1, TILES]], base=0, channel_multiplier=0,
                                 allow_small_or_imprecise_dtypes=True))
            const(nc.gpsimd.iota(free_at[:, :], pattern=[[REGION, E]], base=0, channel_multiplier=0,
                                 allow_small_or_imprecise_dtypes=True))
            const(nc.gpsimd.iota(coef[:, :], pattern=[[REGION, E + 1]], base=0, channel_multiplier=0,
                                 allow_small_or_imprecise_dtypes=True))
            const(nc.gpsimd.iota(rowbuf[:, :, H:H + 1].bitcast(I32), pattern=[[P, 2 * COLS], [0, 1]],
                                 base=-2 * BATCH * N, channel_multiplier=1))
            pool.wait_ge(vconst_done, 1)
            const(nc.gpsimd.iota(template[:, 0, H:H + 1].bitcast(I32), pattern=[[0, 1]], base=TOKENS,
                                 channel_multiplier=1))
            const(nc.gpsimd.iota(template[:, 1, H:H + 1].bitcast(I32), pattern=[[0, 1]], base=TOKENS,
                                 channel_multiplier=1))
            assert done[0] == CONSTS, done

            def root1(g):
                if g.within(GRAPHS):
                    pool.wait_ge(stats1_steps, 4 * (g.i + 1))
                    if g.past(1):
                        pool.wait_ge(root1_steps, 2 * g.i)
                    settle(pool, "pool")
                    nc.gpsimd.tensor_tensor(var1[:, :], mv1[g.slot(2)][:, :, 1], eps[:, :], ALU.add)\
                        .then_inc(root1_steps, 1)
                    pool.wait_ge(root1_steps, 2 * g.i + 1)
                    if g.past(2):
                        pool.wait_ge(nf_ready, 2 * (g.i - 1))
                    settle(pool, "pool")
                    nc.gpsimd.tensor_tensor(rstd1[g.slot(2)][:, :], var1[:, :], minus_half[:, :], ALU.pow)\
                        .then_inc(root1_steps, 1)

            def root2(g):
                if g.within(GRAPHS):
                    pool.wait_ge(stats2_steps, 4 * (g.i + 1))
                    if g.past(1):
                        pool.wait_ge(root2_steps, 2 * g.i)
                    settle(pool, "pool")
                    nc.gpsimd.tensor_tensor(var2[:, :], mv2[g.slot(2)][:, :, 1], eps[:, :], ALU.add)\
                        .then_inc(root2_steps, 1)
                    pool.wait_ge(root2_steps, 2 * g.i + 1)
                    if g.past(2):
                        pool.wait_ge(xn_ready, 2 * (g.i - 1))
                    settle(pool, "pool")
                    nc.gpsimd.tensor_tensor(rstd2[g.slot(2)][:, :], var2[:, :], minus_half[:, :], ALU.pow)\
                        .then_inc(root2_steps, 1)

            def scatter(g):
                if g.within(GRAPHS):
                    pool.wait_ge(xn_ready, 2 * (g.i + 1))
                    pool.wait_ge(place_steps, PLACE * (g.turn(BATCH) + 1))
                    settle(pool, "pool")
                    for r in range(RB):
                        c = RB * g.slot(8) + r
                        for places in (slot_1, slot_2):
                            nc.gpsimd.indirect_dma_start(rows, bass.IndirectOffsetOnAxis(ap=places[:, c:c + 1], axis=0),
                                                         rowbuf[:, c, :], None).then_inc(scatter_done[g.slot(8)], 16)

            def free(g):
                if g.within(GRAPHS - 8):
                    pool.wait_ge(scatter_done[g.slot(8)], 64 * (g.turn(8) + 1))
                    pool.sem_inc(rows_free, 1)

            def tick(k):
                scatter(k.back(14))
                root1(k)
                free(k.back(15))
                root2(k.back(6))
            pool.sem_inc(rows_free, 8)
            ticks(pool, tick)

            for i, s in enumerate(x2_stored):
                pool.wait_ge(s, 16 * GRAPHS // 4)
            pool.wait_ge(trash_zeroed, 16)

            def step(t):
                v = t.back(2)
                if v.within(TILES):
                    pool.wait_ge(yout_ready, 2 * (v.i + 1))
                    pool.wait_ge(tok_copied, v.i + 1)
                    settle(pool, "pool")
                    for s in range(SUB):
                        nc.gpsimd.indirect_dma_start(
                            out, bass.IndirectOffsetOnAxis(ap=place_tok[v.slot(2)][:, s:s + 1], axis=0),
                            yout[v.slot(2)][:, s, :], None, compute_op=ALU.add).then_inc(added, 16)
                        pool.wait_ge(added, 16 * (SUB * v.i + s + 1))
                        settle(pool, "pool")
                if t.within(TILES):
                    pool.wait_ge(xr_in[t.slot(2)], 16 * (t.turn(2) + 1))
                    settle(pool, "pool")
                    nc.gpsimd.tensor_copy(place_tok[t.slot(2)][:, :], xr[t.slot(2)][:, :, H].bitcast(I32))\
                        .then_inc(tok_copied, 1)
            steps(pool, step)

        @block.scalar
        def _(sc):
            nc_act = nc.scalar.activation

            def exps(g):
                if g.within(GRAPHS):
                    sc.wait_ge(rowmax_steps, 5 * (g.i + 1))
                    if g.past(2):
                        sc.wait_ge(probs_turned, g.i - 1)
                    for r in range(RB):
                        nc_act(e1[g.slot(2)][:, r, :], s_ps[:, r, :], ACT.Exp,
                               bias=ebias[g.slot(2)][:, 0, r:r + 1]).then_inc(exp_ready, 1)
                        nc_act(e2[g.slot(2)][:, r, :], s_ps[:, r, :], ACT.Exp,
                               bias=ebias[g.slot(2)][:, 1, r:r + 1], scale=SLOPE).then_inc(exp_ready, 1)

            def normalise(g):
                if g.within(GRAPHS):
                    sc.wait_ge(shift1_ready, g.i + 1)
                    if g.past(4):
                        sc.wait_ge(attn_ready, g.i - 3)
                    p = g.slot(2)
                    for r in range(RB):
                        nc_act(nf[g.slot(4)][:, r, 0:H], xb[g.slot(8)][:, r, :], ACT.Identity,
                               bias=shift1[p][:, r:r + 1], scale=rstd1[p][:, r:r + 1]).then_inc(nf_ready, 1)

            def copy_nfT(g):
                if g.within(GRAPHS):
                    sc.wait_ge(nfT_ready, g.i + 1)
                    if g.past(2):
                        sc.wait_ge(ad_ready, g.i - 1)
                    nc_act(nfT[g.slot(2)], nfT_ps, ACT.Copy).then_inc(nfT_copied, 1)

            def copy_probsT(g):
                if g.within(GRAPHS):
                    sc.wait_ge(probs_turned, g.i + 1)
                    if g.past(2):
                        sc.wait_ge(attn_ready, g.i - 1)
                    nc_act(probsT[g.slot(2)], probsT_ps, ACT.Copy).then_inc(probsT_ready, 1)

            def normalise2(g):
                if g.within(GRAPHS):
                    sc.wait_ge(shift2_ready, g.i + 1)
                    sc.wait_ge(rows_free, g.i + 1)
                    p = g.slot(2)
                    for r in range(RB):
                        nc_act(rowbuf[:, RB * g.slot(8) + r, 0:H], x2[g.slot(4)][:, r, :], ACT.Identity,
                               bias=shift2[p][:, r:r + 1], scale=rstd2[p][:, r:r + 1]).then_inc(xn_ready, 1)

            def copy_xnT(g):
                if g.within(GRAPHS):
                    sc.wait_ge(xnT_ready, g.i + 1)
                    if g.past(2):
                        sc.wait_ge(logits_ready, g.i - 1)
                    nc_act(xnT[g.slot(2)], xnT_ps, ACT.Copy).then_inc(xnT_copied, 1)

            def gate(b):
                sc.wait_ge(choose_steps, CHOOSE * (b + 1))
                nc_act(gate_e[:, :], gate_e[:, :], ACT.Exp).then_inc(gate_exp, 1)

            def split_hi(q):
                sc.wait_ge(w_in[q % 2], 16 * (q // 2 + 1))
                if q // 2 >= 4:
                    sc.wait_ge(plan_steps, PLAN)
                    for s in x2_stored:
                        sc.wait_ge(s, 16 * GRAPHS // 4)
                a = w_at(q // 2, 2 * (q % 2))
                nc_act(W[:, a:a + HALF], stage[q % 2][:, :], ACT.Copy, scale=WSCALE).then_inc(w_hi, 1)

            def tick(k):
                exps(k.back(3))
                b = k.back(13)
                if k.o % BATCH == 1 and b.within(GRAPHS):
                    gate(b.turn(BATCH))
                copy_probsT(k.back(4))
                normalise(k.back(1))
                copy_xnT(k.back(8))
                normalise2(k.back(7))
                copy_nfT(k.back(1))
                if isinstance(k.i, int) and k.i in SPLIT_TICKS:
                    split_hi(SPLIT_TICKS.index(k.i))
            sc.wait_ge(const_steps, 3)
            nc_act(gate_e[:, 0:1], ones[:, 0:1], ACT.Exp).then_inc(passed["act"], 1)
            sc.wait_ge(passed["act"], 1)
            ticks(sc, tick)
            for q in range(DRAIN_SPLITS, STEP_SPLITS[0][0]):
                split_hi(q)

            def x_hi(t):
                if t.within(TILES):
                    sc.wait_ge(xT_ready, t.i + 1)
                    if t.past(2):
                        sc.wait_ge(hidden_ready, 4 * (t.i - 1))
                    nc_act(xTh[t.slot(2)][:, :, :], xT_ps, ACT.Copy).then_inc(xT_hi, 1)

            def silu(t):
                if t.within(TILES):
                    e = sc.value_load(tile_expert[0:1, bass.ds(t.i, 1)], min_val=0, max_val=E - 1)
                    for j in range(4):
                        sc.wait_ge(hidden_ready, 4 * t.i + j + 1)
                        if j > 1 or t.past(1):
                            sc.wait_ge(parts_steps, 2 * (4 * t.i + j - 1))
                        settle(sc, "act")
                        for f in range(2):
                            ins = nc_act(act[j % 2][:, f, :], h_ps[j][:, f, :], ACT.Silu,
                                         bias=b1T[:, bass.ds(e * FT + 2 * j + f, 1)], scale=1.0 / WSCALE)
                        ins.then_inc(silu_ready, 1)

            def weigh(t):
                if t.within(TILES):
                    sc.wait_ge(ysum_ready, t.i + 1)
                    sc.wait_ge(weight_steps, 2 * (t.i + 1))
                    if t.past(2):
                        sc.wait_ge(added, 32 * (t.i - 1))
                    for s in range(SUB):
                        nc_act(yout[t.slot(2)][:, s, :], ysum[t.slot(2)][:, s, :], ACT.Copy,
                               scale=place_w[t.slot(2)][:, s:s + 1]).then_inc(yout_ready, 1)

            sc.wait_ge(b1_ready, 1)
            sc.wait_ge(plan_steps, PLAN)
            nc_act(gate_e[:, 0:1], ones[:, 0:1], ACT.Silu).then_inc(passed["act"], 1)
            x_hi(At(2, 0, 0))

            def step(t):
                weigh(t.back(2))
                silu(t)
                x_hi(t.back(-1))
                if isinstance(t.i, int) and t.i < len(STEP_SPLITS):
                    for q in STEP_SPLITS[t.i]:
                        split_hi(q)
            steps(sc, step)

        @block.vector
        def _(dve):
            v = nc.vector
            v.memset(template[:, :, :], 0.0).then_inc(vconst_done, 1)
            v.memset(ad_bias[:, :, :], 0.0).then_inc(vconst_done, 1)

            def late_constants():
                dve.wait_ge(vconst_done, 2)
                dve.wait_ge(vectors_in, 16 * 8)
                v.tensor_copy(ad_bias[:, :, 0], attn_b_sb[:, 0:1].to_broadcast((P, RB))).then_inc(vconst_done, 1)
                dve.wait_ge(vconst_done, 3)
                dve.wait_ge(const_steps, CONSTS)
                dve.wait_ge(b1_turned, 1)
                v.tensor_copy(b1T[:, :], b1T_ps).then_inc(b1_ready, 1)

            def stats1(g):
                if g.within(GRAPHS):
                    dve.wait_ge(x_in[g.slot(8)], 16 * (g.turn(8) + 1))
                    if g.past(1):
                        dve.wait_ge(stats1_steps, 4 * g.i)
                    for r in range(RB):
                        v.bn_stats(stat1[:, r, :], xb[g.slot(8)][:, r, :]).then_inc(stats1_steps, 1)
                    yield
                    dve.wait_ge(stats1_steps, 4 * g.i + 2)
                    if g.past(2):
                        dve.wait_ge(shift1_ready, g.i - 1)
                    settle(dve, "dve")
                    for r in range(RB):
                        v.bn_aggr(mv1[g.slot(2)][:, r, :], stat1[:, r, :]).then_inc(stats1_steps, 1)

            def stats2(g):
                if g.within(GRAPHS):
                    dve.wait_ge(x2_steps, 3 * (g.i + 1))
                    if g.past(1):
                        dve.wait_ge(stats2_steps, 4 * g.i)
                    for r in range(RB):
                        v.bn_stats(stat2[:, r, :], x2[g.slot(4)][:, r, :]).then_inc(stats2_steps, 1)
                    yield
                    dve.wait_ge(stats2_steps, 4 * g.i + 2)
                    if g.past(2):
                        dve.wait_ge(shift2_ready, g.i - 1)
                    settle(dve, "dve")
                    for r in range(RB):
                        v.bn_aggr(mv2[g.slot(2)][:, r, :], stat2[:, r, :]).then_inc(stats2_steps, 1)

            def shifts1(g):
                if g.within(GRAPHS):
                    dve.wait_ge(root1_steps, 2 * (g.i + 1))
                    if g.past(2):
                        dve.wait_ge(nf_ready, 2 * (g.i - 1))
                    p = g.slot(2)
                    v.scalar_tensor_tensor(out=shift1[p][:, :], in0=mv1[p][:, :, 0], scalar=-1.0, in1=rstd1[p][:, :],
                                           op0=ALU.mult, op1=ALU.mult).then_inc(shift1_ready, 1)

            def shifts2(g):
                if g.within(GRAPHS):
                    dve.wait_ge(root2_steps, 2 * (g.i + 1))
                    if g.past(2):
                        dve.wait_ge(xn_ready, 2 * (g.i - 1))
                    p = g.slot(2)
                    v.scalar_tensor_tensor(out=shift2[p][:, :], in0=mv2[p][:, :, 0], scalar=-1.0, in1=rstd2[p][:, :],
                                           op0=ALU.mult, op1=ALU.mult).then_inc(shift2_ready, 1)

            def mask(g):
                if g.within(GRAPHS):
                    if isinstance(g.i, int) and g.i == 0:
                        dve.wait_ge(const_steps, CONSTS)
                    dve.wait_ge(adj_in[g.slot(4)], 16 * (g.turn(4) + 1))
                    if g.past(2):
                        dve.wait_ge(scores_ready, g.i - 1)
                    v.tensor_tensor(noedge[g.slot(2)], adjb[g.slot(4)], minus_eye[:, :, :], ALU.is_equal)\
                        .then_inc(mask_ready, 1)

            def copy_ad(g):
                if g.within(GRAPHS):
                    dve.wait_ge(ad_ready, g.i + 1)
                    v.tensor_tensor(ad[g.slot(2)][:, :, :], ad_ps, ad_bias[:, :, :], ALU.add).then_inc(ad_copied, 1)

            def spread(g):
                if g.within(GRAPHS):
                    dve.wait_ge(ad_copied, g.i + 1)
                    if g.past(2):
                        dve.wait_ge(scores_ready, g.i - 1)
                    v.tensor_tensor(diag[g.slot(2)], ident[:, :].unsqueeze(1).to_broadcast((P, RB, P)),
                                    ad[g.slot(2)][:, :, 1:2].to_broadcast((P, RB, P)), ALU.mult)\
                        .then_inc(diag_ready, 1)

            def row_max(g):
                if g.within(GRAPHS):
                    a = ad[g.slot(2)][:, :, 0]
                    done = 5 * g.i
                    dve.wait_ge(ad_copied, g.i + 1)
                    dve.wait_ge(scores_ready, g.i + 1)
                    v.tensor_reduce(rmax[:, :], s_ps, AX.X, ALU.max).then_inc(rowmax_steps, 1)
                    yield
                    dve.wait_ge(rowmax_steps, done + 1)
                    v.tensor_tensor(rz[:, :], rmax[:, :], a, ALU.add).then_inc(rowmax_steps, 1)
                    yield
                    dve.wait_ge(rowmax_steps, done + 2)
                    v.scalar_tensor_tensor(out=rm[:, :], in0=rz[:, :], scalar=SLOPE, in1=rz[:, :],
                                           op0=ALU.mult, op1=ALU.max).then_inc(rowmax_steps, 1)
                    yield
                    dve.wait_ge(rowmax_steps, done + 3)
                    if g.past(2):
                        dve.wait_ge(exp_ready, 4 * (g.i - 1))
                    v.tensor_tensor(ebias[g.slot(2)][:, 0, :], a, rm[:, :], ALU.subtract)\
                        .then_inc(rowmax_steps, 1)
                    v.scalar_tensor_tensor(out=ebias[g.slot(2)][:, 1, :], in0=a, scalar=SLOPE, in1=rm[:, :],
                                           op0=ALU.mult, op1=ALU.subtract).then_inc(rowmax_steps, 1)

            def join(g):
                if g.within(GRAPHS):
                    dve.wait_ge(exp_ready, 4 * (g.i + 1))
                    p = g.slot(2)
                    v.tensor_tensor(e1[p], e1[p], e2[p], ALU.max).then_inc(probs_ready, 1)

            def residual(g):
                if g.within(GRAPHS):
                    dve.wait_ge(attn_ready, g.i + 1)
                    if g.past(1):
                        dve.wait_ge(x2_steps, 3 * g.i)
                    v.reciprocal(rinv[:, :], o_ps[:, :, H]).then_inc(x2_steps, 1)
                    yield
                    dve.wait_ge(x2_steps, 3 * g.i + 1)
                    if g.past(4):
                        dve.wait_ge(x2_stored[g.slot(4)], 16 * g.turn(4))
                        dve.wait_ge(xn_ready, 2 * (g.i - 3))
                    for r in range(RB):
                        v.scalar_tensor_tensor(out=x2[g.slot(4)][:, r, :], in0=o_ps[:, r, 0:H], scalar=rinv[:, r:r + 1],
                                               in1=xb[g.slot(8)][:, r, :], op0=ALU.mult, op1=ALU.add)\
                            .then_inc(x2_steps, 1)

            def copy_logits(g):
                if g.within(GRAPHS):
                    dve.wait_ge(logits_ready, g.i + 1)
                    c = RB * g.slot(BATCH)
                    v.tensor_tensor(lg[:, c:c + RB, :], lg_ps, bg_sb[:, :, :], ALU.add).then_inc(logits_copied, 1)

            def over_experts(a):
                return a.unsqueeze(2).to_broadcast((P, COLS, E))

            def choose(b):
                flat = lambda t: t[:, :, :].rearrange("p c e -> p (c e)")
                done = CHOOSE * b
                dve.wait_ge(logits_copied, BATCH * (b + 1))
                v.tensor_reduce(top1[:, :], lg[:, :, :], AX.X, ALU.max).then_inc(choose_steps, 1)
                yield
                dve.wait_ge(choose_steps, done + 1)
                v.tensor_tensor(hit[:, :, :], lg[:, :, :], over_experts(top1[:, :]), ALU.is_equal)\
                    .then_inc(choose_steps, 1)
                yield
                dve.wait_ge(choose_steps, done + 2)
                v.tensor_tensor(hit[:, :, :], hit[:, :, :], rank[:, :, :], ALU.mult).then_inc(choose_steps, 1)
                yield
                dve.wait_ge(choose_steps, done + 3)
                v.tensor_reduce(rank1[:, :], hit[:, :, :], AX.X, ALU.max).then_inc(choose_steps, 1)
                yield
                dve.wait_ge(choose_steps, done + 4)
                v.tensor_tensor(first[:, :, :], rank[:, :, :], over_experts(rank1[:, :]), ALU.is_equal)\
                    .then_inc(choose_steps, 1)
                yield
                dve.wait_ge(choose_steps, done + 5)
                v.scalar_tensor_tensor(out=flat(lg2), in0=flat(first), scalar=-BIG, in1=flat(lg),
                                       op0=ALU.mult, op1=ALU.add).then_inc(choose_steps, 1)
                yield
                dve.wait_ge(choose_steps, done + 6)
                v.tensor_reduce(top2[:, :], lg2[:, :, :], AX.X, ALU.max).then_inc(choose_steps, 1)
                yield
                dve.wait_ge(choose_steps, done + 7)
                v.tensor_tensor(hit[:, :, :], lg2[:, :, :], over_experts(top2[:, :]), ALU.is_equal)\
                    .then_inc(choose_steps, 1)
                yield
                dve.wait_ge(choose_steps, done + 8)
                v.tensor_tensor(hit[:, :, :], hit[:, :, :], rank[:, :, :], ALU.mult).then_inc(choose_steps, 1)
                yield
                dve.wait_ge(choose_steps, done + 9)
                v.tensor_reduce(rank2[:, :], hit[:, :, :], AX.X, ALU.max).then_inc(choose_steps, 1)
                yield
                dve.wait_ge(choose_steps, done + 10)
                v.tensor_tensor(second[:, :, :], rank[:, :, :], over_experts(rank2[:, :]), ALU.is_equal)\
                    .then_inc(choose_steps, 1)
                v.tensor_tensor(gate_e[:, :], top2[:, :], top1[:, :], ALU.subtract).then_inc(choose_steps, 1)
                yield
                dve.wait_ge(choose_steps, done + 12)
                v.tensor_tensor(sel[:, :, :], first[:, :, :], second[:, :, :], ALU.add).then_inc(choose_steps, 1)

            def place(b, half):
                mine = slice(half * COLS, (half + 1) * COLS)
                done = PLACE * b

                def after(n):
                    dve.wait_ge(place_steps, done + n)

                dve.wait_ge(prefix_ready, b + 1)
                dve.wait_ge(choose_steps, CHOOSE * (b + 1))
                v.tensor_tensor(slot_f[:, :, :], pre_ps, free_at[:, :].unsqueeze(1).to_broadcast((P, COLS, E)),
                                ALU.add).then_inc(place_steps, 1)
                dve.wait_ge(gate_exp, b + 1)
                v.tensor_scalar(gate_w1[:, :], gate_e[:, :], 1.0, None, ALU.add).then_inc(place_steps, 1)
                after(1)
                v.tensor_tensor(slot_s[0][:, :, :], slot_f[:, :, :], first[:, :, :], ALU.mult)\
                    .then_inc(place_steps, 1)
                v.tensor_tensor(slot_s[1][:, :, :], slot_f[:, :, :], second[:, :, :], ALU.mult)\
                    .then_inc(place_steps, 1)
                after(2)
                v.reciprocal(gate_w1[:, :], gate_w1[:, :]).then_inc(place_steps, 1)
                after(4)
                v.tensor_reduce(slot_1[:, mine], slot_s[0][:, :, :], AX.X, ALU.add).then_inc(place_steps, 1)
                v.tensor_reduce(slot_2[:, mine], slot_s[1][:, :, :], AX.X, ALU.add).then_inc(place_steps, 1)
                after(5)
                v.tensor_tensor(rowbuf[:, mine, H + 1], gate_e[:, :], gate_w1[:, :], ALU.mult)\
                    .then_inc(place_steps, 1)
                v.tensor_tensor(free_at[:, :], tot_ps, free_at[:, :], ALU.add).then_inc(place_steps, 1)
                v.tensor_copy(rowbuf[:, mine, H + 3], rank1[:, :]).then_inc(place_steps, 1)
                v.tensor_scalar(rowbuf[:, mine, H].bitcast(I32), rowbuf[:, mine, H].bitcast(I32),
                                2 * BATCH * N, None, ALU.add).then_inc(place_steps, 1)
                after(8)
                v.tensor_tensor(rowbuf[:, mine, H + 2], gate_w1[:, :], rowbuf[:, mine, H + 1], ALU.subtract)\
                    .then_inc(place_steps, 1)
                after(PLACE)

            def split_lo(q):
                dve.wait_ge(w_hi, q + 1)
                a = w_at(q // 2, 2 * (q % 2))
                v.scalar_tensor_tensor(out=W[:, a + HALF:a + 2 * HALF], in0=stage[q % 2][:, :], scalar=WSCALE,
                                       in1=W[:, a:a + HALF], op0=ALU.mult, op1=ALU.subtract).then_inc(w_lo, 1)

            def go_on(steps):
                next(steps, None)

            def tick(k):
                b = k.back(12)
                choice = choose(b.turn(BATCH)) if k.o % BATCH == 0 and b.within(GRAPHS) else iter(())
                if isinstance(k.i, int) and k.i == 2:
                    late_constants()
                peak, first_norm = row_max(k.back(3)), stats1(k)
                second_norm, sum_up_x2 = stats2(k.back(6)), residual(k.back(6))
                go_on(peak)
                go_on(sum_up_x2)
                shifts1(k.back(1))
                go_on(sum_up_x2)
                copy_logits(k.back(9))
                go_on(peak)
                go_on(choice)
                shifts2(k.back(7))
                go_on(peak)
                go_on(choice)
                go_on(first_norm)
                go_on(peak)
                go_on(choice)
                copy_ad(k.back(2))
                go_on(first_norm)
                go_on(choice)
                go_on(second_norm)
                spread(k.back(2))
                go_on(choice)
                go_on(second_norm)
                go_on(choice)
                go_on(choice)
                mask(k.back(1))
                go_on(choice)
                join(k.back(3))
                go_on(choice)
                for _ in choice:
                    pass
                b = k.back(13)
                if k.o % BATCH == 1 and b.within(GRAPHS):
                    place(b.turn(BATCH), (b.o // BATCH) % 2)
                if isinstance(k.i, int) and k.i in SPLIT_TICKS:
                    split_lo(SPLIT_TICKS.index(k.i))
            ticks(dve, tick)

            n = [0]

            def link(ins):
                n[0] += 1
                ins.then_inc(plan_steps, 1)
                dve.wait_ge(plan_steps, n[0])

            def over_tiles(a, width):
                return a.unsqueeze(1).to_broadcast((P, TILES, width))

            link(v.tensor_copy(region_end[:, :], free_at[:, :]))
            link(v.tensor_tensor(tiles_f[:, :], free_at[:, :], coef[:, 0:E], ALU.subtract))
            link(v.tensor_scalar(cnt_i[:, :], tiles_f[:, :], float(TILE - 1), None, ALU.add))
            link(v.tensor_scalar(tiles_i[:, :], cnt_i[:, :], TILE.bit_length() - 1, None, ALU.logical_shift_right))
            link(v.tensor_scalar(tiles_f[:, :], tiles_i[:, :], 1.0, None, ALU.max))
            link(v.tensor_tensor_scan(tile_end[:, :], ones[:, 0:E], tiles_f[:, :], 0.0, ALU.mult, ALU.add))
            link(v.tensor_tensor(tiles_f[:, :], tile_end[:, :], tiles_f[:, :], ALU.subtract))
            link(v.scalar_tensor_tensor(out=coef[:, 0:E], in0=tiles_f[:, :], scalar=-float(TILE), in1=coef[:, 0:E],
                                        op0=ALU.mult, op1=ALU.add))
            link(v.memset(coef[:, E:E + 1], 1e6))
            link(v.tensor_tensor(past[:, :, 0:E], over_tiles(tile_end[:, :], E),
                                 tile_no[:, :].unsqueeze(2).to_broadcast((P, TILES, E)), ALU.is_le))
            link(v.tensor_reduce(tile_e[:, :], past[:, :, 0:E], AX.X, ALU.add))
            link(v.tensor_scalar(tile_rank[:, :], tile_e[:, :], -1.0, float(E), ALU.mult, ALU.add))
            link(v.tensor_scalar(tile_expert[:, :], tile_e[:, :], float(E - 1), None, ALU.min))
            link(v.tensor_tensor(past[:, :, :], over_tiles(expert_no[:, :], E + 1),
                                 tile_e[:, :].unsqueeze(2).to_broadcast((P, TILES, E + 1)), ALU.is_equal))
            link(v.tensor_tensor(past[:, :, :], past[:, :, :], over_tiles(coef[:, :], E + 1), ALU.mult))
            link(v.tensor_reduce(tile_b[:, :], past[:, :, :], AX.X, ALU.add))
            link(v.scalar_tensor_tensor(out=tile_b[:, :], in0=tile_no[:, :], scalar=float(TILE), in1=tile_b[:, :],
                                        op0=ALU.mult, op1=ALU.add))
            link(v.tensor_scalar(tile_base[:, :], tile_b[:, :], float(NULL_BASE), None, ALU.min))
            assert n[0] == PLAN, n

            for q in range(DRAIN_SPLITS, STEP_SPLITS[0][0]):
                split_lo(q)

            def x_lo(t):
                if t.within(TILES):
                    dve.wait_ge(xT_hi, t.i + 1)
                    v.tensor_tensor(xTl[t.slot(2)][:, :, :], xT_ps, xTh[t.slot(2)][:, :, :], ALU.subtract)\
                        .then_inc(xT_lo, 1)

            def parts(t):
                if t.within(TILES):
                    hi, lo = hid[t.slot(2)]
                    if t.past(2):
                        dve.wait_ge(y_ready, t.i - 1)
                    for j in range(4):
                        dve.wait_ge(silu_ready, 4 * t.i + j + 1)
                        pair = slice(2 * j, 2 * j + 2)
                        v.tensor_copy(hi[:, pair, :], act[j % 2][:, :, :]).then_inc(parts_steps, 1)
                        dve.wait_ge(parts_steps, 2 * (4 * t.i + j) + 1)
                        v.tensor_tensor(lo[:, pair, :], act[j % 2][:, :, :], hi[:, pair, :], ALU.subtract)\
                            .then_inc(parts_steps, 1)

            def sum_up(t):
                if t.within(TILES):
                    e = dve.value_load(tile_expert[0:1, bass.ds(t.i, 1)], min_val=0, max_val=E - 1)
                    dve.wait_ge(y_ready, t.i + 1)
                    if t.past(2):
                        dve.wait_ge(yout_ready, 2 * (t.i - 1))
                    v.scalar_tensor_tensor(out=ysum[t.slot(2)][:, :, :], in0=y_ps[t.slot(2)], scalar=1.0 / WSCALE,
                                           in1=b2_sb[:, bass.ds(e, 1), :].to_broadcast((P, SUB, H)),
                                           op0=ALU.mult, op1=ALU.add).then_inc(ysum_ready, 1)

            def weights(t):
                if t.within(TILES):
                    r = xr[t.slot(2)]
                    dve.wait_ge(xr_in[t.slot(2)], 16 * (t.turn(2) + 1))
                    if t.past(1):
                        dve.wait_ge(weight_steps, 2 * t.i)
                    v.scalar_tensor_tensor(out=place_q[:, :], in0=r[:, :, H + 3], scalar=tile_rank[:, bass.ds(t.i, 1)],
                                           in1=r[:, :, H + 2], op0=ALU.is_equal, op1=ALU.mult)\
                        .then_inc(weight_steps, 1)
                    dve.wait_ge(weight_steps, 2 * t.i + 1)
                    if t.past(2):
                        dve.wait_ge(yout_ready, 2 * (t.i - 1))
                    v.tensor_tensor(place_w[t.slot(2)][:, :], place_q[:, :], r[:, :, H + 1], ALU.add)\
                        .then_inc(weight_steps, 1)

            x_lo(At(2, 0, 0))

            def step(t):
                sum_up(t.back(2))
                parts(t)
                x_lo(t.back(-1))
                weights(t)
                if isinstance(t.i, int) and t.i < len(STEP_SPLITS):
                    for q in STEP_SPLITS[t.i]:
                        split_lo(q)
            steps(dve, step)

        @block.tensor
        def _(pe):
            mm, tp = nc.tensor.matmul, nc.tensor.transpose
            pe.wait_ge(const_steps, CONSTS)

            def turn_nf(g):
                if g.within(GRAPHS):
                    pe.wait_ge(nf_ready, 2 * (g.i + 1))
                    if g.past(1):
                        pe.wait_ge(nfT_copied, g.i)
                    for r in range(RB):
                        for k in range(KT):
                            ins = tp(nfT_ps[:, k, r * P:(r + 1) * P], nf[g.slot(4)][:, r, k * P:(k + 1) * P],
                                     ident[:, :])
                    ins.then_inc(nfT_ready, 1)

            def attend(g):
                if g.within(GRAPHS):
                    pe.wait_ge(probsT_ready, g.i + 1)
                    if g.past(1):
                        pe.wait_ge(x2_steps, 3 * g.i)
                    for r in range(RB):
                        for j in range(RB):
                            ins = mm(o_ps[:, r, 0:H + 1], probsT[g.slot(2)][:, j, r * P:(r + 1) * P],
                                     nf[g.slot(4)][:, j, 0:H + 1], start=(j == 0), stop=(j == RB - 1))
                    ins.then_inc(attn_ready, 1)

            def node_scores(g):
                if g.within(GRAPHS):
                    pe.wait_ge(nfT_copied, g.i + 1)
                    if g.past(1):
                        pe.wait_ge(ad_copied, g.i)
                    if g.past(7):
                        pe.wait_ge(logits_copied, g.i - 6)
                    for r in range(RB):
                        for k in range(KT):
                            ins = mm(ad_ps[:, r, :], nfT[g.slot(2)][:, k, r * P:(r + 1) * P], w_sd[:, k, :],
                                     start=(k == 0), stop=(k == KT - 1))
                    ins.then_inc(ad_ready, 1)

            def edge_scores(g):
                if g.within(GRAPHS):
                    pe.wait_ge(diag_ready, g.i + 1)
                    pe.wait_ge(mask_ready, g.i + 1)
                    if g.past(1):
                        pe.wait_ge(exp_ready, 4 * g.i)
                    for j in range(RB):
                        mm(s_ps[:, :, j * P:(j + 1) * P], ones[:, :],
                           diag[g.slot(2)][:, j, :].unsqueeze(1).to_broadcast((P, RB, P)), start=(j == 0), stop=False)
                    mm(s_ps, minus_big[:, :], noedge[g.slot(2)], start=False, stop=True).then_inc(scores_ready, 1)

            def turn_probs(g):
                if g.within(GRAPHS):
                    pe.wait_ge(probs_ready, g.i + 1)
                    if g.past(1):
                        pe.wait_ge(probsT_ready, g.i)
                    for r in range(RB):
                        for j in range(RB):
                            ins = tp(probsT_ps[:, j, r * P:(r + 1) * P], e1[g.slot(2)][:, r, j * P:(j + 1) * P],
                                     ident[:, :])
                    ins.then_inc(probs_turned, 1)

            def turn_xn(g):
                if g.within(GRAPHS):
                    pe.wait_ge(xn_ready, 2 * (g.i + 1))
                    if g.past(1):
                        pe.wait_ge(xnT_copied, g.i)
                    for r in range(RB):
                        for k in range(KT):
                            ins = tp(xnT_ps[:, k, r * P:(r + 1) * P],
                                     rowbuf[:, RB * g.slot(8) + r, k * P:(k + 1) * P], ident[:, :])
                    ins.then_inc(xnT_ready, 1)

            def gate_logits(g):
                if g.within(GRAPHS):
                    pe.wait_ge(xnT_copied, g.i + 1)
                    pe.wait_ge(ad_copied, capped(g.i + 7, GRAPHS))
                    if g.past(1):
                        pe.wait_ge(logits_copied, g.i)
                    for r in range(RB):
                        for k in range(KT):
                            ins = mm(lg_ps[:, r, :], xnT[g.slot(2)][:, k, r * P:(r + 1) * P], wg_sb[:, k, :],
                                     start=(k == 0), stop=(k == KT - 1))
                    ins.then_inc(logits_ready, 1)

            def count(b):
                pe.wait_ge(choose_steps, CHOOSE * (b + 1))
                mm(pre_ps, before[:, :], sel[:, :, :], start=True, stop=False)
                for c in range(COLS - 1):
                    mm(pre_ps[:, c + 1:COLS, :], ones_bf[:, :],
                       sel[:, c:c + 1, :].to_broadcast((P, COLS - 1 - c, E)), start=False, stop=(c == COLS - 2))
                for c in range(COLS):
                    ins = mm(tot_ps, ones_bf[:, :], sel[:, c, :], start=(c == 0), stop=(c == COLS - 1))
                ins.then_inc(prefix_ready, 1)

            def tick(k):
                gate_logits(k.back(9))
                b = k.back(13)
                if k.o % BATCH == 1 and b.within(GRAPHS):
                    count(b.turn(BATCH))
                turn_probs(k.back(4))
                turn_xn(k.back(8))
                node_scores(k.back(2))
                attend(k.back(5))
                edge_scores(k.back(2))
                turn_nf(k.back(1))
                if isinstance(k.i, int) and k.i == 1:
                    pe.wait_ge(vectors_in, 16 * 8)
                    tp(b1T_ps, b1_rows[:, :], ident[0:E * FT, 0:E * FT]).then_inc(b1_turned, 1)
                    pe.wait_ge(b1_ready, 1)
            ticks(pe, tick)

            def turn_x(t):
                if t.within(TILES):
                    pe.wait_ge(xr_in[t.slot(2)], 16 * (t.turn(2) + 1))
                    if t.past(1):
                        pe.wait_ge(xT_lo, t.i)
                    for s in range(SUB):
                        for k in range(KT):
                            ins = tp(xT_ps[:, k, s * P:(s + 1) * P], xr[t.slot(2)][:, s, k * P:(k + 1) * P],
                                     ident[:, :])
                    ins.then_inc(xT_ready, 1)

            def hidden(t):
                if t.within(TILES):
                    e = pe.value_load(tile_expert[0:1, bass.ds(t.i, 1)], min_val=0, max_val=E - 1)
                    pe.wait_ge(xT_lo, t.i + 1)
                    if isinstance(t.i, int) and t.i < E:
                        pe.wait_ge(w_lo, 2 * t.i + 1)
                    for j in range(4):
                        if t.past(1):
                            pe.wait_ge(silu_ready, 4 * (t.i - 1) + j + 1)
                        settle(pe, "pe")
                        for f in (2 * j, 2 * j + 1):
                            n = 0
                            for k in range(KT):
                                for part, xT in ((0, xTh), (0, xTl), (1, xTh)):
                                    at = (part * HALF + k * FF + f * P)
                                    ins = mm(h_ps[j][:, f % 2, :], W[:, bass.ds(e * (4 * HALF) + at, P)],
                                             xT[t.slot(2)][:, k, :], start=(n == 0), stop=(n == 5))
                                    n += 1
                        ins.then_inc(hidden_ready, 1)

            def result(t):
                if t.within(TILES):
                    e = pe.value_load(tile_expert[0:1, bass.ds(t.i, 1)], min_val=0, max_val=E - 1)
                    hi, lo = hid[t.slot(2)]
                    if isinstance(t.i, int) and t.i < E:
                        pe.wait_ge(w_lo, 2 * t.i + 2)
                    pe.wait_ge(parts_steps, 8 * (t.i + 1))
                    if t.past(2):
                        pe.wait_ge(ysum_ready, t.i - 1)
                    for s in range(SUB):
                        n = 0
                        for f in range(FT):
                            for src, part in ((hi, 2), (lo, 2), (hi, 3)):
                                at = part * HALF + f * H
                                ins = mm(y_ps[t.slot(2)][:, s, :], src[:, f, s * P:(s + 1) * P],
                                         W[:, bass.ds(e * (4 * HALF) + at, H)], start=(n == 0), stop=(n == 3 * FT - 1))
                                n += 1
                    ins.then_inc(y_ready, 1)

            pe.wait_ge(plan_steps, PLAN)
            turn_x(At(2, 0, 0))

            def step(t):
                hidden(t)
                turn_x(t.back(-1))
                result(t.back(1))
            steps(pe, step)


_INS = ["x", "adj", "L0_gnn_attn_w_src", "L0_gnn_attn_w_dst", "L0_gnn_attn_b", "L0_ffn_Wg", "L0_ffn_bg",
        "L0_ffn_W1", "L0_ffn_b1", "L0_ffn_W2", "L0_ffn_b2"]


def kernel(**inputs):
    import numpy as _np
    import concourse.bacc as _bacc
    from concourse import mybir as _mybir
    from concourse.bass_utils import run_bass_kernel_spmd as _run

    nc = _bacc.Bacc("TRN2", target_bir_lowering=False, num_devices=1)
    arrays, args = {}, []
    for name in _INS:
        a = _np.ascontiguousarray(inputs[name])
        arrays[f"in_{name}_dram"] = a
        args.append(nc.dram_tensor(f"in_{name}_dram", a.shape, _mybir.dt.from_np(a.dtype), kind="ExternalInput").ap())
    out = nc.dram_tensor("out_0_dram", (TOKENS + TRASH, H), F32, kind="ExternalOutput").ap()
    build_gat_moe(nc, *args, out)
    r = _run(nc, [arrays], core_ids=[0])
    return r.results[0]["out_0_dram"][:TOKENS].reshape(GRAPHS, N, H)
```
